# Optimizing a Trainium2 kernel written in Bass

```python
import numpy as np
import jax
import jax.numpy as jnp

def _softmax(x, axis=-1):
    return jax.nn.softmax(x, axis=axis)

def _gelu(x):
    return jax.nn.gelu(x, approximate=True)

def _silu(x):
    return jax.nn.silu(x)

def _sigmoid(x):
    return jax.nn.sigmoid(x)

def _layernorm(x, axis=-1, eps=1e-05):
    m = jnp.mean(x, axis=axis, keepdims=True)
    v = jnp.var(x, axis=axis, keepdims=True)
    return (x - m) / jnp.sqrt(v + eps)

def _scatter_add(tgt, idx, src, axis=0):
    return tgt.at[idx].add(src)

def _segment_sum(src, seg, n):
    return jax.ops.segment_sum(src, seg, n)
kernel_name = 'mk_pixart_resid_d2_seqx_r8_80f8af'

def setup_inputs(seed: int=0):
    np.random.seed(seed)
    _w = jnp.asarray

    def _rec_inputs():
        import jax
        import jax.numpy as jnp
        _rk = jax.random.key(seed)
        x = 7.22e-05 + 1 * jax.random.normal(jax.random.fold_in(_rk, 1), (4, 512, 128), jnp.float32)
        _lenS = 512 - jax.random.randint(jax.random.fold_in(_rk, 7), (4,), 0, max(1, 512 // 4) + 1, jnp.int32)
        _lenS2 = 77 - jax.random.randint(jax.random.fold_in(_rk, 8), (4,), 0, max(1, 77 // 4) + 1, jnp.int32)
        _ctx_1024P = jax.random.normal(jax.random.fold_in(_rk, 11), (4, 16, 128), jnp.float32)
        _ctx_1024c = jax.random.dirichlet(jax.random.fold_in(_rk, 511), 0.3 * jnp.ones((16,), jnp.float32), (4, 77))
        _ctx_1024t = jnp.einsum('bsk,bkd->bsd', _ctx_1024c, _ctx_1024P)
        _ctx_1024t = _ctx_1024t * jax.lax.rsqrt(jnp.mean(jnp.square(_ctx_1024t)) + 1e-12) * 0.953939
        ctx_1024 = 4.13588e-05 + 0.999923 * (_ctx_1024t + 0.3 * jax.random.normal(jax.random.fold_in(_rk, 611), (4, 77, 128), jnp.float32))
        condB_tau = jax.random.uniform(jax.random.fold_in(_rk, 12), (4,), jnp.float32, 0.0, 1.45372)
        fside_BxS2_0 = 0.0088954 + 1.00633 * jax.random.normal(jax.random.fold_in(_rk, 13), (4, 77), jnp.float32)
        return (x, ctx_1024, condB_tau, fside_BxS2_0)
    x, ctx_1024, condB_tau, fside_BxS2_0 = _rec_inputs()

    def _L0_xcond_setup():
        import jax, jax.numpy as jnp
        import numpy as np
        D_MODEL = 128
        N_HEADS = 16
        key = jax.random.key(seed)
        ks = jax.random.split(key, 16)
        B, L, S, D = (4, 256, 256, D_MODEL)
        inp = {'q': jax.random.normal(ks[0], (B, L, D), jnp.float32), 'k': jax.random.normal(ks[1], (B, S, D), jnp.float32), 'v': jax.random.normal(ks[2], (B, S, D), jnp.float32), 'tau': jax.random.uniform(ks[3], (B, 1), jnp.float32, 0.5, 1.5), 'delta': jax.random.normal(ks[4], (B, S), jnp.float32)}
        s = 1.0 / np.sqrt(D)
        inp['Wq'] = jax.random.normal(ks[5], (D, D), jnp.float32) * s
        inp['bq'] = jnp.zeros((D,), jnp.float32)
        inp['Wk'] = jax.random.normal(ks[6], (D, D), jnp.float32) * s
        inp['bk'] = jnp.zeros((D,), jnp.float32)
        inp['Wv'] = jax.random.normal(ks[7], (D, D), jnp.float32) * s
        inp['bv'] = jnp.zeros((D,), jnp.float32)
        inp['Wo'] = jax.random.normal(ks[8], (D, D), jnp.float32) * s
        inp['bo'] = jnp.zeros((D,), jnp.float32)
        return inp
    _L0_xcond_all = _L0_xcond_setup()
    _L0_xcond_in = {k: v for k, v in _L0_xcond_all.items() if k in ('Wq', 'bq', 'Wk', 'bk', 'Wv', 'bv', 'Wo', 'bo')}
    del _L0_xcond_all

    def _L0_ffn_setup():
        import jax, jax.numpy as jnp
        import numpy as np
        D_MODEL, D_FF, RANK = (128, 512, 32)
        B, S = (4, 512)
        key = jax.random.key(seed)
        ks = jax.random.split(key, 7)
        return {'x': jax.random.normal(ks[0], (B, S, D_MODEL), dtype=jnp.float32), 'U1': jax.random.normal(ks[1], (D_MODEL, RANK), dtype=jnp.float32) * 0.02, 'V1': jax.random.normal(ks[2], (RANK, D_FF), dtype=jnp.float32) * 0.02, 'b1': jnp.zeros((D_FF,), dtype=jnp.float32), 'U2': jax.random.normal(ks[3], (D_FF, RANK), dtype=jnp.float32) * 0.02, 'V2': jax.random.normal(ks[4], (RANK, D_MODEL), dtype=jnp.float32) * 0.02, 'b2': jnp.zeros((D_MODEL,), dtype=jnp.float32)}
    _L0_ffn_all = _L0_ffn_setup()
    _L0_ffn_in = {k: v for k, v in _L0_ffn_all.items() if k in ('U1', 'V1', 'b1', 'U2', 'V2', 'b2')}
    del _L0_ffn_all

    def _L1_xcond_setup():
        import jax, jax.numpy as jnp
        import numpy as np
        B, S, D, H = (2, 256, 128, 16)
        DK = D // H

        def _split_heads(x):
            b, s, _ = x.shape
            return x.reshape(b, s, H, DK).transpose(0, 2, 1, 3)
        key = jax.random.key(seed)
        ks = jax.random.split(key, 14)
        inp = {'query': jax.random.normal(ks[0], (B, S, D), jnp.float32), 'key': jax.random.normal(ks[1], (B, S, D), jnp.float32), 'value': jax.random.normal(ks[2], (B, S, D), jnp.float32), 'tau': jax.random.uniform(ks[3], (B, 1), jnp.float32, 0.5, 1.5), 'delta': jax.random.normal(ks[4], (B, S), jnp.float32)}
        sc = 1.0 / np.sqrt(D)
        for i, name in enumerate(['q', 'k', 'v', 'o']):
            inp[f'W{name}'] = jax.random.normal(ks[5 + 2 * i], (D, D), jnp.float32) * sc
            inp[f'b{name}'] = jax.random.normal(ks[6 + 2 * i], (D,), jnp.float32) * 0.01
        return inp
    _L1_xcond_all = _L1_xcond_setup()
    _L1_xcond_in = {k: v for k, v in _L1_xcond_all.items() if k in ('Wq', 'bq', 'Wk', 'bk', 'Wv', 'bv', 'Wo', 'bo')}
    del _L1_xcond_all

    def _L1_ffn_setup():
        import jax, jax.numpy as jnp
        import numpy as np
        TEMPERATURE = 1.0
        TOPK = 2
        key = jax.random.key(seed)
        ks = jax.random.split(key, 6)
        S, B, H, F, E = (256, 4, 128, 512, 8)
        x = jax.random.normal(ks[0], (S, B, H), dtype=jnp.float32)
        gate_w = jax.random.normal(ks[1], (E, H), dtype=jnp.float32) * (1.0 / np.sqrt(H))
        w1 = jax.random.normal(ks[2], (E, H, F), dtype=jnp.float32) * (1.0 / np.sqrt(H))
        b1 = jnp.zeros((E, F), dtype=jnp.float32)
        w2 = jax.random.normal(ks[3], (E, F, H), dtype=jnp.float32) * (1.0 / np.sqrt(F))
        b2 = jnp.zeros((E, H), dtype=jnp.float32)
        return {'x': x, 'gate_w': gate_w, 'w1': w1, 'b1': b1, 'w2': w2, 'b2': b2}
    _L1_ffn_all = _L1_ffn_setup()
    _L1_ffn_in = {k: v for k, v in _L1_ffn_all.items() if k in ('gate_w', 'w1', 'b1', 'w2', 'b2')}
    del _L1_ffn_all
    return {'x': x, 'ctx_1024': ctx_1024, 'condB_tau': condB_tau, 'fside_BxS2_0': fside_BxS2_0, 'L0_xcond_Wq': _L0_xcond_in['Wq'], 'L0_xcond_bq': _L0_xcond_in['bq'], 'L0_xcond_Wk': _L0_xcond_in['Wk'], 'L0_xcond_bk': _L0_xcond_in['bk'], 'L0_xcond_Wv': _L0_xcond_in['Wv'], 'L0_xcond_bv': _L0_xcond_in['bv'], 'L0_xcond_Wo': _L0_xcond_in['Wo'], 'L0_xcond_bo': _L0_xcond_in['bo'], 'L0_ffn_U1': _L0_ffn_in['U1'], 'L0_ffn_V1': _L0_ffn_in['V1'], 'L0_ffn_b1': _L0_ffn_in['b1'], 'L0_ffn_U2': _L0_ffn_in['U2'], 'L0_ffn_V2': _L0_ffn_in['V2'], 'L0_ffn_b2': _L0_ffn_in['b2'], 'L1_xcond_Wq': _L1_xcond_in['Wq'], 'L1_xcond_bq': _L1_xcond_in['bq'], 'L1_xcond_Wk': _L1_xcond_in['Wk'], 'L1_xcond_bk': _L1_xcond_in['bk'], 'L1_xcond_Wv': _L1_xcond_in['Wv'], 'L1_xcond_bv': _L1_xcond_in['bv'], 'L1_xcond_Wo': _L1_xcond_in['Wo'], 'L1_xcond_bo': _L1_xcond_in['bo'], 'L1_ffn_gate_w': _L1_ffn_in['gate_w'], 'L1_ffn_w1': _L1_ffn_in['w1'], 'L1_ffn_b1': _L1_ffn_in['b1'], 'L1_ffn_w2': _L1_ffn_in['w2'], 'L1_ffn_b2': _L1_ffn_in['b2']}

def reference(x, ctx_1024, condB_tau, fside_BxS2_0, L0_xcond_Wq, L0_xcond_bq, L0_xcond_Wk, L0_xcond_bk, L0_xcond_Wv, L0_xcond_bv, L0_xcond_Wo, L0_xcond_bo, L0_ffn_U1, L0_ffn_V1, L0_ffn_b1, L0_ffn_U2, L0_ffn_V2, L0_ffn_b2, L1_xcond_Wq, L1_xcond_bq, L1_xcond_Wk, L1_xcond_bk, L1_xcond_Wv, L1_xcond_bv, L1_xcond_Wo, L1_xcond_bo, L1_ffn_gate_w, L1_ffn_w1, L1_ffn_b1, L1_ffn_w2, L1_ffn_b2):
    import jax
    import jax.numpy as jnp

    def _L0_xcond_ref(q, k, v, tau, delta, Wq, bq, Wk, bk, Wv, bv, Wo, bo):
        import jax, jax.numpy as jnp
        import numpy as np
        D_MODEL = 128
        N_HEADS = 16
        B, L, D = q.shape
        S = k.shape[1]
        H = N_HEADS
        E = D // H
        qh = (q @ Wq.T + bq).reshape(B, L, H, E)
        kh = (k @ Wk.T + bk).reshape(B, S, H, E)
        vh = (v @ Wv.T + bv).reshape(B, S, H, E)
        scale = 1.0 / np.sqrt(E).astype(np.float32)
        scores = jnp.einsum('blhe,bshe->bhls', qh, kh)
        scores = scores * tau[:, None, None, :] + delta[:, None, None, :]
        a = jax.nn.softmax(scale * scores, axis=-1)
        out = jnp.einsum('bhls,bshd->blhd', a, vh).reshape(B, L, D)
        return out @ Wo.T + bo

    def _L0_ffn_ref(x, U1, V1, b1, U2, V2, b2):
        import jax, jax.numpy as jnp
        import numpy as np
        D_MODEL, D_FF, RANK = (128, 512, 32)
        B, S = (4, 512)
        P = jnp.einsum('bsd,dr->bsr', x, U1)
        H = jax.nn.gelu(jnp.einsum('bsr,rf->bsf', P, V1) + b1)
        Q = jnp.einsum('bsf,fr->bsr', H, U2)
        return jnp.einsum('bsr,rd->bsd', Q, V2) + b2

    def _L1_xcond_ref(query, key, value, tau, delta, Wq, bq, Wk, bk, Wv, bv, Wo, bo):
        import jax, jax.numpy as jnp
        import numpy as np
        B, S, D, H = (2, 256, 128, 16)
        DK = D // H

        def _split_heads(x):
            b, s, _ = x.shape
            return x.reshape(b, s, H, DK).transpose(0, 2, 1, 3)
        q = _split_heads(query @ Wq.T + bq)
        k = _split_heads(key @ Wk.T + bk)
        v = _split_heads(value @ Wv.T + bv)
        scores = jnp.einsum('bhqd,bhkd->bhqk', q, k)
        scores = scores * tau[:, :, None, None] + delta[:, None, None, :]
        scores = scores / jnp.sqrt(jnp.asarray(DK, scores.dtype))
        p_attn = jax.nn.softmax(scores, axis=-1)
        x = jnp.einsum('bhqk,bhkd->bhqd', p_attn, v)
        x = x.transpose(0, 2, 1, 3).reshape(query.shape[0], -1, H * DK)
        return x @ Wo.T + bo

    def _L1_ffn_ref(x, gate_w, w1, b1, w2, b2):
        import jax, jax.numpy as jnp
        import numpy as np
        TEMPERATURE = 1.0
        TOPK = 2
        s, b, h = x.shape
        x_flat = x.reshape(s * b, h)
        logits = x_flat @ gate_w.T
        probs = jax.nn.softmax(logits / TEMPERATURE, axis=-1)
        topk_probs, topk_idx = jax.lax.top_k(probs, TOPK)
        hidden = jax.nn.relu(jnp.einsum('th,ehf->tef', x_flat, w1) + b1[None])
        all_out = jnp.einsum('tef,efh->teh', hidden, w2) + b2[None]
        gathered = jnp.take_along_axis(all_out, topk_idx[:, :, None], axis=1)
        y_flat = jnp.sum(gathered * topk_probs[:, :, None], axis=1)
        return y_flat.reshape(s, b, h)
    x = x + _L0_xcond_ref(_layernorm(x, axis=-1), ctx_1024, ctx_1024, condB_tau[:, None], fside_BxS2_0, L0_xcond_Wq, L0_xcond_bq, L0_xcond_Wk, L0_xcond_bk, L0_xcond_Wv, L0_xcond_bv, L0_xcond_Wo, L0_xcond_bo)
    x = x + _L0_ffn_ref(_layernorm(x, axis=-1), L0_ffn_U1, L0_ffn_V1, L0_ffn_b1, L0_ffn_U2, L0_ffn_V2, L0_ffn_b2)
    x = x + _L1_xcond_ref(_layernorm(x, axis=-1), ctx_1024, ctx_1024, condB_tau[:, None], fside_BxS2_0, L1_xcond_Wq, L1_xcond_bq, L1_xcond_Wk, L1_xcond_bk, L1_xcond_Wv, L1_xcond_bv, L1_xcond_Wo, L1_xcond_bo)
    x = x + _L1_ffn_ref(_layernorm(x, axis=-1), L1_ffn_gate_w, L1_ffn_w1, L1_ffn_b1, L1_ffn_w2, L1_ffn_b2)
    return x

_drawn_inputs = setup_inputs


def setup_inputs(seed=0):
    import zlib

    import numpy as np

    out = dict(_drawn_inputs(seed))
    spreads = {'L0_xcond_bq': (0.0, 0.364),
     'L0_xcond_bk': (0.0, 2.0),
     'L0_xcond_bv': (0.0, 0.1),
     'L0_xcond_bo': (0.0, 0.1),
     'L0_ffn_b1': (0.0, 0.8),
     'L0_ffn_b2': (0.0, 0.32),
     'L1_ffn_b1': (0.0, 1.047),
     'L1_ffn_b2': (0.0, 0.737)}
    factors = {'L0_ffn_U1': 8.0,
     'L0_ffn_V1': 8.0,
     'L0_ffn_U2': 8.0,
     'L0_ffn_V2': 8.0,
     'L1_xcond_bq': 64.0,
     'L1_xcond_bk': 64.0,
     'L1_xcond_bv': 19.742,
     'L1_xcond_bo': 23.408}
    for name, (base, spread) in spreads.items():
        noise = np.random.default_rng([zlib.crc32(name.encode()), seed]).standard_normal(out[name].shape)
        drawn = base * np.exp(spread * noise) if base else spread * noise
        out[name] = jnp.asarray(drawn.astype(out[name].dtype))
    for name, factor in factors.items():
        out[name] = (out[name] * factor).astype(out[name].dtype)
    return out
```

```python
from contextlib import ExitStack

import numpy as np
import concourse.bass as bass
from concourse import mybir

LAYERS, BATCH, SEQ, DIM, CTX = 2, 4, 512, 128, 77
HEADS, HEAD_DIM = 16, 8
GROUPS, PER_GROUP = 4, 4
TILES = SEQ // 128
RANK, FF, FF_BLOCKS = 32, 512, 4
EXPERTS, TOPK = 8, 2
CTX_ALL = BATCH * CTX
ONE_ROWS, MAX_ROW = 2, 98
ROUNDS = LAYERS * BATCH
PROB_SLOTS = 10
NUM_STEP, DEN_STEP = 5, 7
INVERT_STEPS = (4, 6, 8, 10)
NORM_STEP = 11
OUT_STEP = 13
STATS_STEP, APPLY_STEP = 14, 15
FRONT_AT = {0: [("tr",)], 1: [("q", 0)], 2: [("q", 1)], 3: [("q", 2)], 4: [("q", 3)], 13: [("mt",)]}
for _step in range(5, 13):
    FRONT_AT[_step] = [("a", (_step - 5) // 2, 2 * ((_step - 5) % 2) + _c) for _c in range(2)]
ROUTE_AT = {0: ["transpose"], 1: ["logits"], 2: ["exp"], 3: ["choose"], 12: ["count"], 13: ["place"]}
LNS = 4 * BATCH
CONST_DMAS, FFN_DMAS, MOE_DMAS = 15, 6, 10
TOKENS = BATCH * SEQ
TOKEN_TILES = BATCH * TILES
REGION = TOKENS + 128
ROW = DIM + 2
BLOCKS = TOKENS * TOPK // 128 + EXPERTS
SPARE = BLOCKS - TOKENS * TOPK // 128
UNROLL = 8
SLOTS = 4
STACK = 96 + ONE_ROWS + HEADS
SCALE = 1.0 / float(np.sqrt(np.float32(HEAD_DIM)))
LN_EPS = 1e-5


def pixart_blocks(nc, io, out, debug=None):
    f32, f32r = mybir.dt.float32, mybir.dt.float32r
    ACT, ALU, AX = mybir.ActivationFunctionType, mybir.AluOpType, mybir.AxisListType

    with ExitStack() as ctx:
        def sb(name, shape, dt=f32):
            return ctx.enter_context(nc.sbuf_tensor(name, shape, dt))

        def sem(name):
            return ctx.enter_context(nc.semaphore(name))

        ident = sb("ident", [128, 128])
        ctx_t = sb("ctx_t", [128, CTX_ALL])
        wq = sb("wq", [128, LAYERS, GROUPS, 128])
        wk = sb("wk", [128, LAYERS, GROUPS, 128])
        wv = sb("wv", [128, LAYERS, 128])
        wo = sb("wo", [128, LAYERS, 128])
        bq = sb("bq", [128, LAYERS, GROUPS])
        bk = sb("bk", [128, LAYERS, GROUPS])
        bv = sb("bv", [128, LAYERS, 128])
        bo = sb("bo", [128, LAYERS, 128])
        member = sb("member", [128, PER_GROUP])
        tau = sb("tau", [128, BATCH])
        delta = sb("delta", [128, CTX_ALL])
        delta_hi = sb("delta_hi", [128, CTX_ALL])
        delta_rows = sb("delta_rows", [128, CTX_ALL], f32r)
        low_row = sb("low_row", [128, 1])
        ones_v = sb("ones_v", [128, PER_GROUP, 32])
        x = sb("x", [128, BATCH, TILES, DIM])
        xb = sb("xb", [128, BATCH, TILES, DIM])
        xn = sb("xn", [128, 2, TILES, DIM])
        xt = sb("xt", [128, 2, SEQ])
        ln_stats = sb("ln_stats", [128, 3, TILES, 6])
        ln_mv = sb("ln_mv", [128, 3, TILES, 2])
        ln_var = sb("ln_var", [128, 3, TILES])
        ln_rstd = sb("ln_rstd", [128, 3, TILES])
        minus_half = sb("minus_half", [128, TILES])
        qs = sb("qs", [128, 2, GROUPS, SEQ], f32r)
        ks = sb("ks", [128, BATCH, GROUPS, PER_GROUP, CTX], f32r)
        vm = sb("vm", [128, BATCH, HEADS, 32])
        maxima = sb("maxima", [128, 2, TILES, 128])
        probs = sb("probs", [128, PROB_SLOTS, SEQ])
        rden = sb("rden", [128, SEQ])
        ot = sb("ot", [128, SEQ])
        u1 = sb("u1", [128, 128])
        v1 = sb("v1", [128, FF])
        v1hi = sb("v1hi", [128, FF])
        v1s = sb("v1s", [128, FF], f32r)
        u2 = sb("u2", [128, FF_BLOCKS, RANK])
        v2 = sb("v2", [128, 128])
        b1 = sb("b1", [128, FF_BLOCKS])
        b2 = sb("b2", [128, 128])
        pstack = sb("pstack", [128, SEQ], f32r)
        hid = sb("hid", [128, 2, FF_BLOCKS, SEQ])
        q4 = sb("q4", [128, SEQ])
        kf = sb("kf", [128, GROUPS, CTX_ALL])
        kr = sb("kr", [128, GROUPS, CTX_ALL])

        gate = sb("gate", [128, EXPERTS])
        w1 = sb("w1", [128, EXPERTS * FF])
        w2 = sb("w2", [128, EXPERTS * FF_BLOCKS * DIM])
        e_b1 = sb("e_b1", [128, EXPERTS * FF_BLOCKS])
        e_b2 = sb("e_b2", [128, EXPERTS * DIM])
        before = sb("before", [128, 128])
        all_ones = sb("all_ones", [128, 128])
        tie = sb("tie", [128, EXPERTS * EXPERTS])
        iota = sb("iota", [1, 3 * BLOCKS + 16])
        ids = sb("ids", [128, TOKEN_TILES, TOPK])
        xm = sb("xm", [128, TILES, DIM])
        xtm = sb("xtm", [128, SEQ])
        lmax = sb("lmax", [128, TILES])
        logit = sb("logit", [128, TILES, EXPERTS])
        expl = sb("expl", [128, TILES, EXPERTS])
        rsum = sb("rsum", [128, 2, TILES])
        prob = sb("prob", [128, TILES, EXPERTS])
        greater = sb("greater", [128, TILES, EXPERTS, EXPERTS])
        equal = sb("equal", [128, TILES, EXPERTS, EXPERTS])
        rank = sb("rank", [128, TILES, EXPERTS])
        chosen = sb("chosen", [128, 2, TOPK + 1, TILES, EXPERTS])
        picked = sb("picked", [128, TILES, EXPERTS])
        weight = sb("weight", [128, TOKEN_TILES, TOPK])
        offset = sb("offset", [128, TOKEN_TILES + 1, EXPERTS])
        place = sb("place", [128, TILES, EXPERTS])
        slot_f = sb("slot_f", [128, TILES, TOPK])
        slots = sb("slots", [128, TOKEN_TILES, TOPK], mybir.dt.int32)
        counts = sb("counts", [1, EXPERTS])
        blk_cmp = sb("blk_cmp", [1, EXPERTS, 16])
        blk_end = sb("blk_end", [1, EXPERTS])
        ended = sb("ended", [1, BLOCKS, EXPERTS])
        ended_at = sb("ended_at", [1, BLOCKS, EXPERTS])
        blk_f = sb("blk_f", [1, 4, BLOCKS])
        turn_f = sb("turn_f", [1, BLOCKS // UNROLL])
        turn_i = sb("turn_i", [1, BLOCKS // UNROLL], mybir.dt.int32)
        turn_last = sb("turn_last", [1, BLOCKS // UNROLL], mybir.dt.int32)
        turn_experts = sb("turn_experts", [1, BLOCKS // UNROLL], mybir.dt.int32)
        blk_row = sb("blk_row", [1, BLOCKS], mybir.dt.int32)
        pad_at = sb("pad_at", [1, EXPERTS], mybir.dt.int32)
        rows = sb("rows", [128, SLOTS, ROW])
        goes_to = sb("goes_to", [128, UNROLL], mybir.dt.uint32)
        xs = sb("xs", [128, 2, 128])
        spare = hid[:].rearrange("p h i n -> p (h i n)")
        rows_out_size = 2 * TILES * TOPK * ROW
        rows_out = spare[:, 0:rows_out_size].rearrange("p (h t k r) -> p h t k r", h=2, t=TILES, k=TOPK)
        yt = probs[:, 0:2 * TILES * TOPK * DIM // SEQ].rearrange("p (h s) n -> p h (s n)", h=2)
        zs = spare[:, rows_out_size:rows_out_size + 2 * FF].rearrange("p (h f) -> p h f", h=2)
        ht = probs[:, 4:6].rearrange("p h (i n) -> p h i n", i=FF_BLOCKS)
        ys = probs[:, 6:8].rearrange("p s (u d) -> p (s u) d", u=UNROLL // 2)
        sorted_rows = nc.dram_tensor("sorted_rows", [EXPERTS * REGION + SPARE * 128, ROW], f32, kind="Internal").ap()
        results = nc.dram_tensor("results", [TOKENS * TOPK + (EXPERTS + SPARE) * 128, DIM], f32, kind="Internal").ap()

        ring = ctx.enter_context(nc.psum_tensor("ring", [128, 2, 512], f32))
        sc = ctx.enter_context(nc.psum_tensor("sc", [128, 2, 512], f32))
        num = ctx.enter_context(nc.psum_tensor("num", [128, 2, 512], f32))
        den = ctx.enter_context(nc.psum_tensor("den", [128, 2, 512], f32))

        const_in = sem("const_in")
        x_in = [sem(f"x_in{b}") for b in range(BATCH)]
        ffn_in = sem("ffn_in")
        sel_in = sem("sel_in")
        delta_rep = sem("delta_rep")
        max_rep = sem("max_rep")
        x_out = sem("x_out")
        ones_set = sem("ones_set")
        vm_zero = sem("vm_zero")
        delta_scaled = sem("delta_scaled")
        delta_split = sem("delta_split")
        k_scaled = sem("k_scaled")
        k_split = sem("k_split")
        k_low = sem("k_low")
        ks_done = sem("ks_done")
        stats_done = sem("stats_done")
        mv_done = sem("mv_done")
        var_done = sem("var_done")
        rstd_done = sem("rstd_done")
        xn_done = sem("xn_done")
        q_high = sem("q_high")
        scores_ready = sem("scores_ready")
        exp_done = sem("exp_done")
        den_ready = sem("den_ready")
        rden_done = sem("rden_done")
        ot_done = sem("ot_done")
        xb_done = sem("xb_done")
        v1_split = sem("v1_split")
        p_high = sem("p_high")
        h_ready = sem("h_ready")
        h_done = sem("h_done")
        moe_in = sem("moe_in")
        rows_copied = sem("rows_copied")
        chain_done = sem("chain_done")
        centred = sem("centred")
        exp_logit = sem("exp_logit")
        selected = sem("selected")
        placed = sem("placed")
        rows_sent = sem("rows_sent")
        pads_sent = sem("pads_sent")
        table_done = sem("table_done")
        rows_in = [sem(f"rows_in{u}") for u in range(SLOTS)]
        x_ready = sem("x_ready")
        xs_done = sem("xs_done")
        z_ready = sem("z_ready")
        zs_done = sem("zs_done")
        zt_ready = sem("zt_ready")
        ht_done = sem("ht_done")
        y_ready = sem("y_ready")
        ys_done = sem("ys_done")
        ys_sent = [sem(f"ys_sent{u}") for u in range(UNROLL)]
        yt_in = [sem(f"yt_in{b}") for b in range(BATCH)]
        first_added = sem("first_added")
        x_final = sem("x_final")
        ring_full = [sem(f"ring_full{i}") for i in range(2)]
        ring_drained = [sem(f"ring_drained{i}") for i in range(2)]

        def front_uses(r, step):
            return [(w[0], r, *w[1:]) for w in FRONT_AT.get(step, [])]

        def setup_uses(l):
            return [("k", l, c) for c in range(GROUPS)] + [("v", l, b) for b in range(BATCH)]

        def routing(r, step):
            return [(stage, r - BATCH - 2) for stage in ROUTE_AT.get(step, []) if r >= BATCH + 2]

        def route_uses(stage, b):
            name = {"transpose": "rt", "logits": "rl", "count": "rc"}.get(stage)
            return [(name, b)] if name else []

        LATE = [(stage, b) for b in (BATCH - 2, BATCH - 1) for step in sorted(ROUTE_AT) for stage in ROUTE_AT[step]]

        uses = setup_uses(0)
        for l in range(LAYERS):
            for step in range(HEADS):
                uses += front_uses(BATCH * l, step)
            for b in range(BATCH):
                r = BATCH * l + b
                for step in range(HEADS):
                    if b + 1 < BATCH:
                        uses += front_uses(r + 1, step)
                    if step == OUT_STEP and b:
                        uses.append(("o", r - 1))
                    uses += [u for stage, rb in routing(r, step) for u in route_uses(stage, rb)]
            uses.append(("o", BATCH * l + BATCH - 1))
            if l == 0:
                uses += setup_uses(1) + [("ftr", 0), ("fp", 0)]
                for b in range(BATCH):
                    if b + 1 < BATCH:
                        uses += [("ftr", b + 1), ("fp", b + 1)]
                    uses += [("fq", b), ("fo", b)]
        late_uses = [u for stage, b in LATE for u in route_uses(stage, b)]
        uses = uses[:-1] + late_uses[:3] + uses[-1:] + late_uses[3:]
        at = {u: i for i, u in enumerate(uses)}

        def bank(*u):
            return ring[:, at[u] % 2, :]

        def wait_full(eng, *u):
            eng.wait_ge(ring_full[at[u] % 2], at[u] // 2 + 1)

        def wait_drained(eng, *u):
            eng.wait_ge(ring_drained[at[u] % 2], at[u] // 2 + 1)

        def wait_bank(eng, *u):
            if at[u] >= 2:
                eng.wait_ge(ring_drained[at[u] % 2], at[u] // 2)

        def fills(ins, *u):
            ins.then_inc(ring_full[at[u] % 2], 1)

        def drains(ins, *u):
            ins.then_inc(ring_drained[at[u] % 2], 1)

        def hbank(i):
            return sc[:, i] if i < 2 else num[:, i - 2]

        def ln_of_round(r):
            return r if r < BATCH else r + BATCH

        def wait_x(eng, n):
            kind, b = n // BATCH, n % BATCH
            if kind == 0:
                eng.wait_ge(x_in[b], 16)
            elif kind == 1:
                wait_drained(eng, "o", b)
            elif kind == 2:
                wait_drained(eng, "fo", b)
            else:
                wait_drained(eng, "o", BATCH + b)

        def ln_slot(n):
            return n % 2 if n < 3 * BATCH else 2

        def wait(eng, semaphore, value):
            if not isinstance(value, int) or value > 0:
                eng.wait_ge(semaphore, value)

        def experts_of(eng, turn):
            packed = eng.value_load(turn_experts[0:1, bass.ds(turn, 1)], min_val=0, max_val=(1 << 3 * UNROLL + 6) - 1)
            return {u: (packed >> 3 * (u % (UNROLL + 2))) & (EXPERTS - 1) for u in range(-2, UNROLL)}

        TURNS = BLOCKS // UNROLL

        block = ctx.enter_context(nc.Block())

        @block.sync
        def _(sp):
            sp.dma_start(ident[:], io["ident"]).then_inc(const_in, 16)
            sp.dma_start(x[:, 0], io["x"][0]).then_inc(x_in[0], 16)
            sp.dma_start(ctx_t[:], io["ctx_t"]).then_inc(const_in, 16)
            sp.dma_start(wk[:], io["wk"]).then_inc(const_in, 16)
            sp.dma_start(bk[:], io["bk"]).then_inc(const_in, 16)
            sp.dma_start(tau[:], io["tau"].to_broadcast([128, BATCH])).then_inc(const_in, 16)
            sp.dma_start(delta[96:98, :], io["delta"].to_broadcast([2, CTX_ALL])).then_inc(const_in, 16)
            sp.dma_start(low_row[96:98, :], io["low_row"]).then_inc(const_in, 16)
            sp.dma_start(member[:], io["member"]).then_inc(const_in, 16)
            sp.dma_start(wq[:], io["wq"]).then_inc(const_in, 16)
            sp.dma_start(bq[:], io["bq"]).then_inc(const_in, 16)
            sp.dma_start(wv[:], io["wv"]).then_inc(const_in, 16)
            sp.dma_start(bv[:], io["bv"]).then_inc(const_in, 16)
            sp.dma_start(ones_v[:], io["ones_v"]).then_inc(const_in, 16)
            sp.dma_start(wo[:], io["wo"]).then_inc(const_in, 16)
            sp.dma_start(bo[:], io["bo"]).then_inc(const_in, 16)
            for b in range(1, BATCH):
                sp.dma_start(x[:, b], io["x"][b]).then_inc(x_in[b], 16)
            sp.dma_start(u1[:], io["u1"]).then_inc(ffn_in, 16)
            sp.dma_start(v1[0:96, :], io["v1"]).then_inc(ffn_in, 16)
            sp.dma_start(u2[:], io["u2"]).then_inc(ffn_in, 16)
            sp.dma_start(v2[:], io["v2"]).then_inc(ffn_in, 16)
            sp.dma_start(b1[:], io["b1"]).then_inc(ffn_in, 16)
            sp.dma_start(b2[:], io["b2"]).then_inc(ffn_in, 16)
            sp.dma_start(offset[:, 0], io["regions"]).then_inc(moe_in, 16)
            for name, tile in (("gate", gate), ("before", before), ("tie", tie), ("iota", iota), ("e_b1", e_b1),
                               ("e_b2", e_b2), ("w1", w1), ("w2", w2)):
                sp.dma_start(tile[:], io[name]).then_inc(moe_in, 16)
            sp.dma_start(ids[:], io["ids"]).then_inc(moe_in, 16)
            sp.wait_ge(delta_split, 2)
            for b in range(BATCH):
                src = delta_rows[96:98, b * CTX:(b + 1) * CTX].bitcast(f32).unsqueeze(1).to_broadcast([2, HEADS, CTX])
                sp.dma_start(ks[96:98, b].bitcast(f32).rearrange("p c j k -> p (c j) k"), src).then_inc(delta_rep, 16)
            sp.dma_start(sorted_rows[EXPERTS * REGION:, :], io["pad_rows"][EXPERTS * 128:]).then_inc(pads_sent, 16)
            for r in range(ROUNDS):
                wait_drained(sp, "mt", r)
                src = qs[96:128, r % 2, 0, :].bitcast(f32).unsqueeze(1).to_broadcast([32, GROUPS - 1, SEQ])
                sp.dma_start(qs[96:128, r % 2, 1:GROUPS, :].bitcast(f32), src).then_inc(max_rep, 16)
            sp.wait_ge(table_done, 1)
            for e in range(EXPERTS):
                at_row = sp.value_load(pad_at[0:1, e:e + 1], min_val=0, max_val=EXPERTS * REGION + (SPARE - 1) * 128)
                sp.dma_start(sorted_rows[bass.ds(at_row, 128), :], io["pad_rows"][128 * e:128 * e + 128]).then_inc(pads_sent, 16)
            sp.wait_ge(pads_sent, 16 * (EXPERTS + 1))
            sp.wait_ge(rows_sent, 16 * TOKEN_TILES * TOPK)

            def load_blocks(turn):
                for u in range(UNROLL):
                    n = turn * UNROLL + u
                    first = sp.value_load(blk_row[0:1, bass.ds(n, 1)], min_val=0, max_val=EXPERTS * REGION + (SPARE - 1) * 128)
                    wait(sp, xs_done, n - SLOTS + 1)
                    sp.dma_start(rows[:, u % SLOTS], sorted_rows[bass.ds(first, 128), :]).then_inc(rows_in[u % SLOTS], 16)

            load_blocks(0)
            with sp.Fori(1, TURNS) as turn:
                load_blocks(turn)
            for u in range(UNROLL):
                sp.wait_ge(ys_sent[u], 16 * TURNS)
            for b in range(BATCH):
                if b >= 2:
                    sp.wait_ge(x_final, b - 1)
                src = results[2 * SEQ * b:2 * SEQ * (b + 1), :].rearrange("(p m) d -> p (m d)", p=128)
                sp.dma_start(yt[:, b % 2], src).then_inc(yt_in[b], 16)
            for b in range(BATCH):
                sp.wait_ge(x_final, b + 1)
                sp.dma_start(out[b], x[:, b]).then_inc(x_out, 16)
            sp.wait_ge(x_out, 16 * BATCH)

        @block.gpsimd
        def _(pool):
            pool.dma_start(ks[98:114], io["minus_sel"]).then_inc(sel_in, 16)
            nc.gpsimd.memset(maxima[:, :, :, 96:98], 1.0).then_inc(ones_set, 1)
            nc.gpsimd.memset(maxima[:, :, :, 0:96], 0.0).then_inc(ones_set, 1)
            nc.gpsimd.memset(maxima[:, :, :, 98:128], 0.0).then_inc(ones_set, 1)
            nc.gpsimd.memset(minus_half[:], -0.5).then_inc(ones_set, 1)
            nc.gpsimd.memset(all_ones[:], 1.0).then_inc(ones_set, 1)
            pool.wait_ge(ones_set, 5)
            nc.gpsimd.memset(qs[96:128, 0].bitcast(f32), 1.0).then_inc(ones_set, 1)
            nc.gpsimd.memset(qs[96:128, 1].bitcast(f32), 1.0).then_inc(ones_set, 1)
            pool.wait_ge(ones_set, 7)
            nc.gpsimd.memset(probs[64:128], 0.0).then_inc(ones_set, 1)
            pool.wait_ge(ones_set, 8)
            nc.gpsimd.memset(vm[:], 0.0).then_inc(vm_zero, 1)
            pool.wait_ge(vm_zero, 1)
            def row_copies(b):
                if b >= 2:
                    pool.wait_ge(rows_sent, 16 * TILES * TOPK * (b - 1))
                if b == 0:
                    pool.wait_ge(moe_in, 16 * MOE_DMAS)
                pool.wait_ge(xn_done, 3 * BATCH + b + 1)
                for k in range(TOPK):
                    nc.gpsimd.tensor_copy(rows_out[:, b % 2, :, k, 0:DIM], xm[:])
                nc.gpsimd.tensor_copy(rows_out[:, b % 2, :, :, DIM:DIM + 1],
                                      ids[:, TILES * b:TILES * b + TILES].unsqueeze(3)).then_inc(rows_copied, 1)

            def scatter_rows(b):
                pool.wait_ge(rows_copied, b + 1)
                pool.wait_ge(placed, b + 1)
                for t in range(TILES):
                    for k in range(TOPK):
                        to = slots[:, TILES * b + t, k:k + 1].bitcast(mybir.dt.uint32)
                        pool.indirect_dma_start(out=sorted_rows, out_offset=bass.IndirectOffsetOnAxis(ap=to, axis=0),
                                                in_=rows_out[:, b % 2, t, k], in_offset=None).then_inc(rows_sent, 16)

            for n in range(LNS):
                s, b = ln_slot(n), n % BATCH
                pool.wait_ge(mv_done, n + 1)
                nc.gpsimd.tensor_scalar(ln_var[:, s], ln_mv[:, s, :, 1], LN_EPS, None, ALU.add).then_inc(var_done, 1)
                pool.wait_ge(var_done, n + 1)
                nc.gpsimd.tensor_tensor(ln_rstd[:, s], ln_var[:, s], minus_half[:], ALU.pow).then_inc(rstd_done, 1)
                if n < 3 * BATCH:
                    if n == 0:
                        pool.wait_ge(const_in, 16 * CONST_DMAS)
                    if n == BATCH:
                        pool.wait_ge(ffn_in, 16 * FFN_DMAS)
                    wait_x(pool, n)
                    bias = b2[:, :] if n // BATCH == 1 else bo[:, n // (2 * BATCH), :]
                    nc.gpsimd.tensor_tensor(xb[:, b], x[:, b], bias.unsqueeze(1).to_broadcast([128, TILES, DIM]),
                                            ALU.add).then_inc(xb_done, 1)
                else:
                    if b == 0:
                        wait_full(pool, "fq", BATCH - 1)
                        nc.gpsimd.memset(rows_out[:, :, :, :, DIM:ROW], 0.0).then_inc(ones_set, 1)
                        pool.wait_ge(ones_set, 9)
                    row_copies(b)
                    if b:
                        scatter_rows(b - 1)
            scatter_rows(BATCH - 1)

            for n in range(BLOCKS):
                u = n % UNROLL
                pool.wait_ge(ys_done, n + 1)
                pool.indirect_dma_start(out=results, out_offset=bass.IndirectOffsetOnAxis(ap=goes_to[:, u:u + 1], axis=0),
                                        in_=ys[:, u], in_offset=None).then_inc(ys_sent[u], 16)

        @block.scalar
        def _(act):
            def front(r, step):
                s, l = r % 2, r // BATCH
                for what, *which in FRONT_AT.get(step, []):
                    if what == "tr":
                        wait_full(act, "tr", r)
                        drains(nc.scalar.activation(xt[:, s], bank("tr", r), ACT.Identity), "tr", r)
                    elif what == "q":
                        c, = which
                        wait_full(act, "q", r, c)
                        nc.scalar.activation(qs[0:96, s, c], bank("q", r, c)[0:96], ACT.Identity,
                                             bias=bq[0:96, l, c:c + 1]).then_inc(q_high, 1)
                    elif what == "mt":
                        wait_full(act, "mt", r)
                        drains(nc.scalar.activation(qs[96:128, s, 0], bank("mt", r)[96:128], ACT.Identity), "mt", r)

            def keys(l):
                for c in range(GROUPS):
                    wait_full(act, "k", l, c)
                    if l:
                        act.wait_ge(k_low, l)
                    drains(nc.scalar.activation(kf[:, c], bank("k", l, c)[:, 0:CTX_ALL], ACT.Identity,
                                                bias=bk[:, l, c:c + 1]), "k", l, c)

            def hidden_in(b):
                wait_full(act, "ftr", b)
                drains(nc.scalar.activation(xt[:, b % 2], bank("ftr", b), ACT.Identity), "ftr", b)
                wait_full(act, "fp", b)
                if b:
                    act.wait_ge(h_ready, FF_BLOCKS * b)
                nc.scalar.activation(pstack[0:96], bank("fp", b)[0:96], ACT.Identity).then_inc(p_high, 1)

            def route(stage, b):
                if stage == "transpose":
                    wait_full(act, "rt", b)
                    drains(nc.scalar.activation(xtm[:], bank("rt", b), ACT.Identity), "rt", b)
                elif stage == "exp":
                    wait_drained(act, "rl", b)
                    nc.scalar.activation(expl[:], logit[:], ACT.Exp).then_inc(exp_logit, 1)

            def hidden_blocks(turn):
                e = experts_of(act, turn)
                for u in range(UNROLL):
                    n = turn * UNROLL + u
                    act.wait_ge(zt_ready, n + 1)
                    wait(act, y_ready, n - 1)
                    for i in range(FF_BLOCKS):
                        ins = nc.scalar.activation(ht[:, u % 2, i], den[:, u % 2, 128 * i:128 * i + 128], ACT.Relu,
                                                   bias=e_b1[:, bass.ds(e[u] * FF_BLOCKS + i, 1)])
                    ins.then_inc(ht_done, 1)

            act.wait_ge(const_in, 16 * CONST_DMAS)
            act.wait_ge(ones_set, 8)
            keys(0)
            for l in range(LAYERS):
                for step in range(HEADS):
                    front(BATCH * l, step)
                for b in range(BATCH):
                    r = BATCH * l + b
                    for step in range(HEADS):
                        g = HEADS * r + step
                        act.wait_ge(scores_ready, g + 1)
                        if g >= PROB_SLOTS:
                            last = g - PROB_SLOTS
                            act.wait_ge(den_ready, last // GROUPS + 1)
                        nc.scalar.activation(probs[0:CTX, g % PROB_SLOTS], sc[0:CTX, g % 2], ACT.Exp).then_inc(exp_done, 1)
                        if b + 1 < BATCH:
                            front(r + 1, step)
                        for stage, rb in routing(r, step):
                            route(stage, rb)
                if l == 0:
                    keys(1)
                    act.wait_ge(ffn_in, 16 * FFN_DMAS)
                    hidden_in(0)
                    for b in range(BATCH):
                        for i in range(FF_BLOCKS):
                            act.wait_ge(h_ready, FF_BLOCKS * b + i + 1)
                            if b >= 2 and i == 0:
                                wait_full(act, "fq", b - 2)
                            nc.scalar.activation(hid[:, b % 2, i], hbank(i), ACT.Gelu_apprx_tanh,
                                                 bias=b1[:, i:i + 1]).then_inc(h_done, 1)
                        if b + 1 < BATCH:
                            hidden_in(b + 1)
            for stage, b in LATE:
                route(stage, b)
            act.wait_ge(table_done, 1)
            hidden_blocks(0)
            with act.Fori(1, TURNS) as turn:
                hidden_blocks(turn)

        @block.vector
        def _(dve):
            def ln_stats_of(n):
                s, b = ln_slot(n), n % BATCH
                wait_x(dve, n)
                for t in range(TILES):
                    nc.vector.bn_stats(ln_stats[:, s, t], x[:, b, t]).then_inc(stats_done, 1)
                for t in range(TILES):
                    dve.wait_ge(stats_done, TILES * n + t + 1)
                    ins = nc.vector.bn_aggr(ln_mv[:, s, t], ln_stats[:, s, t])
                ins.then_inc(mv_done, 1)

            def ln_apply(n, reader):
                s, b = ln_slot(n), n % BATCH
                out = xn[:, s] if n < 3 * BATCH else xm
                dve.wait_ge(rstd_done, n + 1)
                if reader:
                    wait_full(dve, *reader)
                for t in range(TILES):
                    ins = nc.vector.tensor_scalar(out[:, t], x[:, b, t], ln_mv[:, s, t, 0:1], ln_rstd[:, s, t:t + 1],
                                                  ALU.subtract, ALU.mult)
                ins.then_inc(xn_done, 1)

            def front(r, step):
                s, l = r % 2, r // BATCH
                for what, *which in FRONT_AT.get(step, []):
                    if what == "q":
                        c, = which
                        dve.wait_ge(q_high, GROUPS * r + c + 1)
                        drains(nc.vector.scalar_tensor_tensor(
                            out=qs[64:96, s, c], in0=bank("q", r, c)[64:96], scalar=bq[64:96, l, c:c + 1],
                            in1=qs[64:96, s, c].bitcast(f32), op0=ALU.add, op1=ALU.subtract), "q", r, c)
                    elif what == "a":
                        t, c = which
                        if r >= 2 and t == 0 and c == 0:
                            wait_full(dve, "mt", r - 2)
                        wait_full(dve, "a", r, t, c)
                        src = bank("a", r, t, c)[:, 0:PER_GROUP * CTX].rearrange("p (j k) -> p j k", k=CTX)
                        col = MAX_ROW + PER_GROUP * c
                        drains(nc.vector.tensor_reduce(maxima[:, s, t, col:col + PER_GROUP], src, AX.X, ALU.max),
                               "a", r, t, c)

            def invert(r, quarter):
                if quarter == 0:
                    dve.wait_ge(den_ready, PER_GROUP * (r + 1))
                part = slice(128 * quarter, 128 * quarter + 128)
                nc.vector.reciprocal(rden[:, part], den[:, r % 2, part]).then_inc(rden_done, 1)

            def normalise(r):
                dve.wait_ge(rden_done, 4 * (r + 1))
                nc.vector.tensor_tensor(ot[:], num[:, r % 2], rden[:], ALU.mult).then_inc(ot_done, 1)

            def residual(r):
                dve.wait_ge(xb_done, ln_of_round(r) + 1)
                wait_full(dve, "o", r)
                b = r % BATCH
                drains(nc.vector.tensor_tensor(x[:, b].rearrange("p t d -> p (t d)"), bank("o", r),
                                               xb[:, b].rearrange("p t d -> p (t d)"), ALU.add), "o", r)

            def keys_split(l):
                for c in range(GROUPS):
                    wait_drained(dve, "k", l, c)
                k4 = kf[0:96].rearrange("p c (b k) -> p c b k", b=BATCH)
                for c in range(GROUPS):
                    ins = nc.vector.scalar_tensor_tensor(
                        out=k4[:, c], in0=k4[:, c], scalar=SCALE,
                        in1=tau[0:96].unsqueeze(2).to_broadcast([96, BATCH, CTX]), op0=ALU.mult, op1=ALU.mult)
                ins.then_inc(k_scaled, 1)
                dve.wait_ge(k_scaled, l + 1)
                if l:
                    dve.wait_ge(ks_done, PER_GROUP * l)
                nc.vector.tensor_copy(kr[0:96].bitcast(f32r), kf[0:96]).then_inc(k_split, 1)
                dve.wait_ge(k_split, l + 1)
                nc.vector.tensor_tensor(kr[32:64].bitcast(f32r), kf[32:64], kr[32:64], ALU.subtract).then_inc(k_low, 1)

            def keys_spread(l, j):
                dve.wait_ge(k_low, l + 1)
                for b in range(BATCH):
                    ins = nc.vector.tensor_scalar(
                        ks[0:96, b, :, j], kr[0:96].rearrange("p c (b k) -> p b c k", b=BATCH)[:, b],
                        member[0:96, j:j + 1], None, ALU.mult)
                ins.then_inc(ks_done, 1)

            def values_in(l):
                dve.wait_ge(vm_zero, 1)
                for b in range(BATCH):
                    wait_full(dve, "v", l, b)
                    for j in range(PER_GROUP):
                        o = vm[0:CTX, b, j::PER_GROUP, 8 * j:8 * j + 8]
                        i0 = bank("v", l, b)[0:CTX, 0:128].rearrange("p (c j d) -> p c j d", c=GROUPS, j=PER_GROUP)[:, :, j]
                        i1 = bv[0:CTX, l].rearrange("p (c j d) -> p c j d", c=GROUPS, j=PER_GROUP)[:, :, j]
                        ins = nc.vector.tensor_tensor(o, i0, i1, ALU.add)
                    drains(ins, "v", l, b)

            chain = [0]

            def chained(ins):
                chain[0] += 1
                ins.then_inc(chain_done, 1)
                dve.wait_ge(chain_done, chain[0])

            def route_norm(b, part):
                if part == 0:
                    ln_stats_of(3 * BATCH + b)
                else:
                    if b:
                        dve.wait_ge(rows_copied, b)
                    ln_apply(3 * BATCH + b, ("rt", b - 1) if b else None)

            def route(stage, b):
                V = nc.vector
                tiles = slice(TILES * b, TILES * b + TILES)
                over = lambda ap: ap.unsqueeze(2).to_broadcast([128, TILES, EXPERTS])
                if stage == "logits":
                    wait_full(dve, "rl", b)
                    lg = bank("rl", b)[:, 0:TILES * EXPERTS].rearrange("p (t e) -> p t e", t=TILES)
                    chained(V.tensor_reduce(lmax[:], lg, AX.X, ALU.max))
                    drains(V.tensor_tensor(logit[:], lg, over(lmax[:]), ALU.subtract), "rl", b)
                elif stage == "choose":
                    dve.wait_ge(exp_logit, b + 1)
                    chained(V.tensor_reduce(rsum[:, 0], expl[:], AX.X, ALU.add))
                    chained(V.reciprocal(rsum[:, 1], rsum[:, 0]))
                    chained(V.tensor_tensor(prob[:], expl[:], over(rsum[:, 1]), ALU.mult))
                    own = prob[:].unsqueeze(3).to_broadcast([128, TILES, EXPERTS, EXPERTS])
                    other = prob[:].unsqueeze(2).to_broadcast([128, TILES, EXPERTS, EXPERTS])
                    V.tensor_tensor(greater[:], other, own, ALU.is_gt)
                    chained(V.tensor_tensor(equal[:], other, own, ALU.is_equal))
                    flat = lambda t: t[:].rearrange("p t a b -> p t (a b)")
                    chained(V.tensor_tensor(flat(equal), flat(equal),
                                            tie[:].unsqueeze(1).to_broadcast([128, TILES, EXPERTS * EXPERTS]), ALU.mult))
                    chained(V.tensor_tensor(flat(greater), flat(greater), flat(equal), ALU.add))
                    chained(V.tensor_reduce(rank[:], greater[:], AX.X, ALU.add))
                    if b >= 2:
                        wait_drained(dve, "rc", b - 2)
                    for k in range(TOPK):
                        V.tensor_scalar(chosen[:, b % 2, k], rank[:], float(k), None, ALU.is_equal)
                    V.tensor_scalar(chosen[:, b % 2, TOPK], rank[:], float(TOPK), None, ALU.is_lt).then_inc(selected, 1)
                    dve.wait_ge(selected, b + 1)
                    for k in range(TOPK):
                        chained(V.tensor_tensor(picked[:], chosen[:, b % 2, k], prob[:], ALU.mult))
                        chained(V.tensor_reduce(weight[:, tiles, k], picked[:], AX.X, ALU.add))
                elif stage == "place":
                    wait_full(dve, "rc", b)
                    cnt = bank("rc", b)
                    totals = cnt[:, TILES * EXPERTS:2 * TILES * EXPERTS].rearrange("p (t e) -> p t e", t=TILES)
                    for t in range(TILES):
                        i = TILES * b + t
                        chained(V.tensor_tensor(offset[:, i + 1], totals[:, t], offset[:, i], ALU.add))
                    drains(V.tensor_tensor(place[:], cnt[:, 0:TILES * EXPERTS].rearrange("p (t e) -> p t e", t=TILES),
                                           offset[:, tiles], ALU.add), "rc", b)
                    wait_drained(dve, "rc", b)
                    for k in range(TOPK):
                        chained(V.tensor_tensor(picked[:], chosen[:, b % 2, k], place[:], ALU.mult))
                        chained(V.tensor_reduce(slot_f[:, :, k], picked[:], AX.X, ALU.add))
                    V.tensor_copy(slots[:, tiles], slot_f[:]).then_inc(placed, 1)

            def block_table():
                V = nc.vector
                last = offset[0:1, TOKEN_TILES]
                block_no, block_row, digit = (iota[:, i * BLOCKS:(i + 1) * BLOCKS] for i in range(3))
                whole = iota[:, 3 * BLOCKS:]
                V.tensor_copy(pad_at[:], last)
                chained(V.tensor_tensor(counts[:], last, offset[0:1, 0], ALU.subtract))
                chained(V.tensor_tensor(blk_cmp[:], counts[:].unsqueeze(2).to_broadcast([1, EXPERTS, 16]),
                                        whole.unsqueeze(1).to_broadcast([1, EXPERTS, 16]), ALU.is_gt))
                chained(V.tensor_reduce(blk_end[:], blk_cmp[:], AX.X, ALU.add))
                for e in range(1, EXPERTS):
                    chained(V.tensor_tensor(blk_end[:, e:e + 1], blk_end[:, e:e + 1], blk_end[:, e - 1:e], ALU.add))
                ends = blk_end[:].unsqueeze(1).to_broadcast([1, BLOCKS, EXPERTS])
                chained(V.tensor_tensor(ended[:], block_no.unsqueeze(2).to_broadcast([1, BLOCKS, EXPERTS]), ends, ALU.is_ge))
                chained(V.tensor_tensor(ended_at[:], ended[:], ends, ALU.mult))
                V.tensor_reduce(blk_f[:, 0], ended[:], AX.X, ALU.add)
                chained(V.tensor_reduce(blk_f[:, 1], ended_at[:], AX.X, ALU.max))
                V.tensor_scalar(blk_f[:, 2], blk_f[:, 0], float(EXPERTS - 1), None, ALU.min)
                chained(V.scalar_tensor_tensor(out=blk_f[:, 3], in0=blk_f[:, 1], scalar=-128.0, in1=block_row,
                                               op0=ALU.mult, op1=ALU.add))
                chained(V.scalar_tensor_tensor(out=blk_f[:, 1], in0=blk_f[:, 0], scalar=float(REGION), in1=blk_f[:, 3],
                                               op0=ALU.mult, op1=ALU.add))
                chained(V.tensor_tensor(blk_f[:, 2], blk_f[:, 2], digit, ALU.mult))
                chained(V.tensor_reduce(turn_f[:], blk_f[:, 2].rearrange("p (t u) -> p t u", u=UNROLL), AX.X, ALU.add))
                chained(V.tensor_copy(turn_i[:], turn_f[:]))
                V.tensor_copy(turn_experts[:, 0:1], turn_i[:, 0:1])
                chained(V.tensor_scalar(turn_last[:, 1:], turn_i[:, :-1], 3 * (UNROLL - 2), 3 * UNROLL,
                                        ALU.logical_shift_right, ALU.logical_shift_left))
                chained(V.tensor_tensor(turn_experts[:, 1:], turn_i[:, 1:], turn_last[:, 1:], ALU.bitwise_or))
                V.tensor_copy(blk_row[:], blk_f[:, 1]).then_inc(table_done, 1)

            def take_up(n, u, turn):
                wait(dve, ys_sent[u], 16 * turn)
                dve.wait_ge(x_ready, n + 1)
                nc.vector.tensor_copy(goes_to[:, u:u + 1], rows[:, u % SLOTS, DIM:DIM + 1].bitcast(mybir.dt.uint32))
                wait(dve, z_ready, n - 1)
                nc.vector.tensor_copy(xs[:, u % 2], ring[:, u % 2, 0:128]).then_inc(xs_done, 1)

            def evacuate(n, u):
                dve.wait_ge(z_ready, n + 1)
                wait(dve, zt_ready, n - 1)
                nc.vector.tensor_copy(zs[:, u % 2], num[:, u % 2]).then_inc(zs_done, 1)

            def finish(n, u, e):
                dve.wait_ge(y_ready, n + 1)
                nc.vector.tensor_tensor(ys[:, u], sc[:, u % 2, 0:DIM], e_b2[:, bass.ds(e * DIM, DIM)],
                                        ALU.add).then_inc(ys_done, 1)

            def moe_blocks(turn, first=False, last=False):
                n0 = turn * UNROLL
                e = experts_of(dve, turn)
                for u in range(UNROLL):
                    if not (last and u == UNROLL - 1):
                        take_up(n0 + u + 1, (u + 1) % UNROLL, turn + (u + 1) // UNROLL)
                    evacuate(n0 + u, u)
                    if not (first and u < 2):
                        finish(n0 + u - 2, (u - 2) % UNROLL, e[u - 2])
                return e

            for n in range(2):
                ln_stats_of(n)
            for n in range(2):
                ln_apply(n, None)
            dve.wait_ge(const_in, 16 * CONST_DMAS)
            dve.wait_ge(ones_set, 7)
            nc.vector.tensor_scalar(delta[96:98], delta[96:98], SCALE, None, ALU.mult).then_inc(delta_scaled, 1)
            dve.wait_ge(delta_scaled, 1)
            nc.vector.tensor_copy(delta_hi[96:98].bitcast(f32r), delta[96:98]).then_inc(delta_split, 1)
            dve.wait_ge(delta_split, 1)
            nc.vector.scalar_tensor_tensor(out=delta_rows[96:98], in0=delta_hi[96:98], scalar=low_row[96:98, 0:1],
                                           in1=delta[96:98], op0=ALU.mult, op1=ALU.add).then_inc(delta_split, 1)
            keys_split(0)
            for j in range(PER_GROUP):
                keys_spread(0, j)
            values_in(0)
            for l in range(LAYERS):
                for step in range(HEADS):
                    front(BATCH * l, step)
                for b in range(BATCH):
                    r = BATCH * l + b
                    for step in range(HEADS):
                        if b + 1 < BATCH:
                            front(r + 1, step)
                        if step in INVERT_STEPS and b:
                            invert(r - 1, INVERT_STEPS.index(step))
                        if step == NORM_STEP and b:
                            normalise(r - 1)
                        for stage, rb in routing(r, step):
                            route(stage, rb)
                        if step == OUT_STEP and b:
                            residual(r - 1)
                        n = ln_of_round(r + 2)
                        if b + 2 < BATCH and step == STATS_STEP:
                            ln_stats_of(n)
                        if b + 2 < BATCH and step == APPLY_STEP:
                            ln_apply(n, ("tr", r))
                        if l == 1 and b and step == STATS_STEP:
                            route_norm(b - 1, 0)
                        if l == 1 and b and step == APPLY_STEP:
                            route_norm(b - 1, 1)
                r = BATCH * l + BATCH - 1
                if l == 0:
                    ln_stats_of(BATCH)
                    ln_stats_of(BATCH + 1)
                    ln_apply(BATCH, ("tr", 2))
                    ln_apply(BATCH + 1, ("tr", 3))
                for quarter in range(4):
                    invert(r, quarter)
                normalise(r)
                if l == 1:
                    for stage, b in LATE[:6]:
                        route(stage, b)
                residual(r)
                if l == 0:
                    keys_split(1)
                    values_in(1)
                    dve.wait_ge(ffn_in, 16 * FFN_DMAS)
                    nc.vector.tensor_copy(v1hi[0:96].bitcast(f32r), v1[0:96]).then_inc(v1_split, 1)
                    nc.vector.tensor_copy(v1s[0:96], v1[0:96]).then_inc(v1_split, 1)
                    dve.wait_ge(v1_split, 2)
                    nc.vector.tensor_tensor(v1s[32:64], v1[32:64], v1hi[32:64], ALU.subtract).then_inc(v1_split, 1)

                    def ffn_low(b):
                        dve.wait_ge(p_high, b + 1)
                        drains(nc.vector.tensor_tensor(pstack[64:96], bank("fp", b)[64:96],
                                                       pstack[64:96].bitcast(f32), ALU.subtract), "fp", b)

                    ffn_low(0)
                    for b in range(BATCH):
                        if b + 1 < BATCH:
                            ffn_low(b + 1)
                        if b + 2 < BATCH:
                            ln_stats_of(BATCH + b + 2)
                            ln_apply(BATCH + b + 2, ("ftr", b))
                        keys_spread(1, b)
                        wait_full(dve, "fq", b)
                        drains(nc.vector.tensor_copy(q4[:], bank("fq", b)), "fq", b)
                        dve.wait_ge(xb_done, BATCH + b + 1)
                        wait_full(dve, "fo", b)
                        drains(nc.vector.tensor_tensor(x[:, b].rearrange("p t d -> p (t d)"), bank("fo", b),
                                                       xb[:, b].rearrange("p t d -> p (t d)"), ALU.add), "fo", b)
                        if b == 1 or b == 2:
                            ln_stats_of(2 * BATCH + b - 1)
                            ln_apply(2 * BATCH + b - 1, ("ftr", b + 1))
            route_norm(BATCH - 1, 0)
            route_norm(BATCH - 1, 1)
            for stage, b in LATE[6:]:
                route(stage, b)
            block_table()
            take_up(0, 0, 0)
            moe_blocks(0, first=True)
            with dve.Fori(1, TURNS - 1) as turn:
                moe_blocks(turn)
            e = moe_blocks(TURNS - 1, last=True)
            for u in (UNROLL - 2, UNROLL - 1):
                finish(BLOCKS - UNROLL + u, u, e[u])
            for b in range(BATCH):
                dve.wait_ge(yt_in[b], 16)
                for t in range(TILES):
                    for k in range(TOPK):
                        y = yt[:, b % 2, (TOPK * t + k) * DIM:(TOPK * t + k + 1) * DIM]
                        ins = nc.vector.scalar_tensor_tensor(out=x[:, b, t], in0=y, scalar=weight[:, TILES * b + t, k:k + 1],
                                                             in1=x[:, b, t], op0=ALU.mult, op1=ALU.add)
                        if k == 0:
                            ins.then_inc(first_added, 1)
                            dve.wait_ge(first_added, TILES * b + t + 1)
                ins.then_inc(x_final, 1)

        @block.tensor
        def _(pe):
            def transposes(src, *u):
                for t in range(TILES):
                    ins = nc.tensor.transpose(bank(*u)[:, 128 * t:128 * t + 128], src[:, t], ident[:])
                fills(ins, *u)

            def front(r, step):
                s, l, b = r % 2, r // BATCH, r % BATCH
                for what, *which in FRONT_AT.get(step, []):
                    if what == "tr":
                        pe.wait_ge(xn_done, ln_of_round(r) + 1)
                        wait_bank(pe, "tr", r)
                        transposes(xn[:, s], "tr", r)
                    elif what == "q":
                        c, = which
                        if c == 0:
                            wait_drained(pe, "tr", r)
                        wait_bank(pe, "q", r, c)
                        fills(nc.tensor.matmul(bank("q", r, c), wq[:, l, c], xt[:, s], start=True, stop=True), "q", r, c)
                    elif what == "a":
                        t, c = which
                        if t == 0:
                            wait_drained(pe, "q", r, c)
                        wait_bank(pe, "a", r, t, c)
                        fills(nc.tensor.matmul(bank("a", r, t, c)[:, 0:PER_GROUP * CTX],
                                               qs[0:98, s, c, 128 * t:128 * t + 128],
                                               ks[0:98, b, c].rearrange("p j k -> p (j k)"),
                                               start=True, stop=True), "a", r, t, c)
                    else:
                        wait_drained(pe, "a", r, TILES - 1, GROUPS - 1)
                        wait_bank(pe, "mt", r)
                        transposes(maxima[:, s], "mt", r)

            def scores(r, step):
                s, l, b, g = r % 2, r // BATCH, r % BATCH, HEADS * r + step
                j, c = step // GROUPS, step % GROUPS
                if step == 0:
                    wait_drained(pe, "mt", r)
                if step == 1:
                    pe.wait_ge(max_rep, 16 * (r + 1))
                if g >= 2:
                    pe.wait_ge(exp_done, g - 1)
                nc.tensor.matmul(sc[0:CTX, g % 2], ks[0:STACK, b, c, j], qs[0:STACK, s, c],
                                 start=True, stop=True).then_inc(scores_ready, 1)

            def values(r, j, which):
                l, b, g = r // BATCH, r % BATCH, HEADS * r + GROUPS * j
                if which == "num":
                    if j == 0 and r >= 2:
                        pe.wait_ge(ot_done, r - 1)
                    pe.wait_ge(exp_done, g + GROUPS)
                for c in range(GROUPS):
                    out = (num if which == "num" else den)[32 * c:32 * c + 32, r % 2]
                    w = vm[:, b, PER_GROUP * c + j] if which == "num" else ones_v[:, j]
                    ins = nc.tensor.matmul(out, w, probs[:, (g + c) % PROB_SLOTS], start=(j == 0),
                                           stop=(j == PER_GROUP - 1), tile_position=(0, 32 * c))
                if which == "den":
                    ins.then_inc(den_ready, 1)

            def values_at(r, step):
                for which, lag in (("num", NUM_STEP), ("den", DEN_STEP)):
                    if (step - lag) % GROUPS == 0:
                        j = (step - lag) // GROUPS
                        if j >= 0:
                            values(r, j, which)
                        elif r % BATCH:
                            values(r - 1, PER_GROUP + j, which)

            def output(r):
                pe.wait_ge(ot_done, r + 1)
                wait_bank(pe, "o", r)
                for t in range(TILES):
                    ins = nc.tensor.matmul(bank("o", r)[:, 128 * t:128 * t + 128], ot[:, 128 * t:128 * t + 128],
                                           wo[:, r // BATCH], start=True, stop=True)
                fills(ins, "o", r)

            def route(stage, b):
                if stage == "transpose":
                    pe.wait_ge(xn_done, 3 * BATCH + b + 1)
                    wait_bank(pe, "rt", b)
                    transposes(xm, "rt", b)
                elif stage == "logits":
                    if b == 0:
                        pe.wait_ge(moe_in, 16 * MOE_DMAS)
                    wait_drained(pe, "rt", b)
                    wait_bank(pe, "rl", b)
                    for t in range(TILES):
                        ins = nc.tensor.matmul(bank("rl", b)[:, EXPERTS * t:EXPERTS * t + EXPERTS],
                                               xtm[:, 128 * t:128 * t + 128], gate[:], start=True, stop=True)
                    fills(ins, "rl", b)
                elif stage == "count":
                    pe.wait_ge(selected, b + 1)
                    wait_bank(pe, "rc", b)
                    either = chosen[:, b % 2, TOPK].rearrange("p t e -> p (t e)")
                    nc.tensor.matmul(bank("rc", b)[:, 0:TILES * EXPERTS], before[:], either, start=True, stop=True)
                    fills(nc.tensor.matmul(bank("rc", b)[:, TILES * EXPERTS:2 * TILES * EXPERTS], all_ones[:], either,
                                           start=True, stop=True), "rc", b)

            def turn_rows(n, u, turn):
                pe.wait_ge(rows_in[u % SLOTS], 16 * (turn * (UNROLL // SLOTS) + u // SLOTS + 1))
                wait(pe, xs_done, n - 1)
                nc.tensor.transpose(ring[:, u % 2, 0:128], rows[:, u % SLOTS, 0:DIM], ident[:]).then_inc(x_ready, 1)

            def first_product(n, u, e):
                pe.wait_ge(xs_done, n + 1)
                wait(pe, zs_done, n - 1)
                nc.tensor.matmul(num[:, u % 2], xs[:, u % 2], w1[:, bass.ds(e * FF, FF)], start=True,
                                 stop=True).then_inc(z_ready, 1)

            def turn_hidden(n, u):
                pe.wait_ge(zs_done, n + 1)
                wait(pe, ht_done, n - 1)
                for i in range(FF_BLOCKS):
                    ins = nc.tensor.transpose(den[:, u % 2, 128 * i:128 * i + 128], zs[:, u % 2, 128 * i:128 * i + 128],
                                              ident[:])
                ins.then_inc(zt_ready, 1)

            def second_product(n, u, e):
                pe.wait_ge(ht_done, n + 1)
                wait(pe, ys_done, n - 1)
                for i in range(FF_BLOCKS):
                    ins = nc.tensor.matmul(sc[:, u % 2, 0:DIM], ht[:, u % 2, i], w2[:, bass.ds(e * FF + i * DIM, DIM)],
                                           start=(i == 0), stop=(i == FF_BLOCKS - 1))
                ins.then_inc(y_ready, 1)

            def moe_blocks(turn, first=False, last=False):
                n0 = turn * UNROLL
                e = experts_of(pe, turn)
                for u in range(UNROLL):
                    first_product(n0 + u, u, e[u])
                    if not (last and u == UNROLL - 1):
                        turn_rows(n0 + u + 1, (u + 1) % UNROLL, turn + (u + 1) // UNROLL)
                    if not (first and u == 0):
                        turn_hidden(n0 + u - 1, (u - 1) % UNROLL)
                    if not (first and u < 2):
                        second_product(n0 + u - 2, (u - 2) % UNROLL, e[u - 2])
                return e

            def keys_values(l):
                for c in range(GROUPS):
                    wait_bank(pe, "k", l, c)
                    fills(nc.tensor.matmul(bank("k", l, c)[:, 0:CTX_ALL], wk[:, l, c], ctx_t[:],
                                           start=True, stop=True), "k", l, c)
                for b in range(BATCH):
                    wait_bank(pe, "v", l, b)
                    fills(nc.tensor.matmul(bank("v", l, b)[0:CTX, 0:128], ctx_t[:, b * CTX:(b + 1) * CTX], wv[:, l],
                                           start=True, stop=True), "v", l, b)

            pe.wait_ge(const_in, 16 * CONST_DMAS)
            keys_values(0)
            pe.wait_ge(sel_in, 16)
            pe.wait_ge(delta_rep, 16 * BATCH)
            pe.wait_ge(ones_set, 7)
            for l in range(LAYERS):
                for step in range(HEADS):
                    if step == 5:
                        pe.wait_ge(ks_done, PER_GROUP * (l + 1))
                    front(BATCH * l, step)
                for b in range(BATCH):
                    r = BATCH * l + b
                    for step in range(HEADS):
                        scores(r, step)
                        if b + 1 < BATCH:
                            front(r + 1, step)
                        values_at(r, step)
                        if step == OUT_STEP and b:
                            output(r - 1)
                        for stage, rb in routing(r, step):
                            route(stage, rb)
                r = BATCH * l + BATCH - 1
                values(r, PER_GROUP - 1, "num")
                values(r, PER_GROUP - 1, "den")
                if l == 1:
                    for stage, b in LATE[:6]:
                        route(stage, b)
                output(r)
                if l == 0:
                    def ffn_first(b):
                        pe.wait_ge(xn_done, BATCH + b + 1)
                        wait_bank(pe, "ftr", b)
                        transposes(xn[:, b % 2], "ftr", b)
                        wait_drained(pe, "ftr", b)
                        wait_bank(pe, "fp", b)
                        fills(nc.tensor.matmul(bank("fp", b), u1[:], xt[:, b % 2], start=True, stop=True), "fp", b)

                    keys_values(1)
                    pe.wait_ge(ffn_in, 16 * FFN_DMAS)
                    pe.wait_ge(v1_split, 3)
                    pe.wait_ge(exp_done, HEADS * BATCH)
                    ffn_first(0)
                    for b in range(BATCH):
                        wait_drained(pe, "fp", b)
                        for i in range(FF_BLOCKS):
                            if b:
                                pe.wait_ge(h_done, FF_BLOCKS * (b - 1) + i + 1)
                            nc.tensor.matmul(hbank(i), v1s[0:96, 128 * i:128 * i + 128], pstack[0:96],
                                             start=True, stop=True).then_inc(h_ready, 1)
                        if b + 1 < BATCH:
                            ffn_first(b + 1)
                        wait_bank(pe, "fq", b)
                        pe.wait_ge(h_done, FF_BLOCKS * (b + 1))
                        for i in range(FF_BLOCKS):
                            ins = nc.tensor.matmul(bank("fq", b)[32 * i:32 * i + 32], u2[:, i], hid[:, b % 2, i],
                                                   start=True, stop=True, tile_position=(0, 32 * i))
                        fills(ins, "fq", b)
                        wait_drained(pe, "fq", b)
                        wait_bank(pe, "fo", b)
                        for t in range(TILES):
                            ins = nc.tensor.matmul(bank("fo", b)[:, 128 * t:128 * t + 128], q4[:, 128 * t:128 * t + 128],
                                                   v2[:], start=True, stop=True)
                        fills(ins, "fo", b)
                    pe.wait_ge(h_done, FF_BLOCKS * BATCH)
            for stage, b in LATE[6:]:
                route(stage, b)
            pe.wait_ge(table_done, 1)
            turn_rows(0, 0, 0)
            moe_blocks(0, first=True)
            with pe.Fori(1, TURNS - 1) as turn:
                moe_blocks(turn)
            e = moe_blocks(TURNS - 1, last=True)
            turn_hidden(BLOCKS - 1, UNROLL - 1)
            for u in (UNROLL - 2, UNROLL - 1):
                second_product(BLOCKS - UNROLL + u, u, e[u])


def arrays_for(inputs):
    a = {k: np.asarray(v) for k, v in inputs.items()}
    rep = {}
    cols = np.array([[8 * (PER_GROUP * c) + i % 32 for i in range(128)] for c in range(GROUPS)])
    def stacked(l, name):
        w = a[f"L{l}_xcond_W{name}"]
        return w[cols].transpose(2, 0, 1)
    def stacked_bias(l, name):
        return a[f"L{l}_xcond_b{name}"][cols].T
    rows = lambda v: np.broadcast_to(v, (128, v.shape[-1]))
    L = range(LAYERS)
    rep["ident"] = np.eye(128, dtype=np.float32)
    rep["x"] = a["x"].reshape(BATCH, 128, TILES, DIM)
    rep["ctx_t"] = a["ctx_1024"].reshape(CTX_ALL, DIM).T
    rep["tau"] = a["condB_tau"].reshape(1, BATCH)
    rep["delta"] = a["fside_BxS2_0"].reshape(1, CTX_ALL)
    rep["low_row"] = np.array([[0.0], [-1.0]], np.float32)
    j = (np.arange(128) % 32) // 8
    rep["member"] = (j[:, None] == np.arange(PER_GROUP)[None]).astype(np.float32)
    rep["ones_v"] = (np.arange(128) < CTX)[:, None, None] * np.broadcast_to(((np.arange(32) // 8)[None] == np.arange(PER_GROUP)[:, None]), (128, PER_GROUP, 32)).astype(np.float32)
    sel = -(np.arange(HEADS)[:, None] == np.arange(HEADS)[None]).astype(np.float32)
    rep["minus_sel"] = np.broadcast_to(sel.reshape(HEADS, 1, GROUPS, PER_GROUP, 1), (HEADS, BATCH, GROUPS, PER_GROUP, CTX))
    rep["wq"] = np.stack([stacked(l, "q") for l in L], 1)
    rep["wk"] = np.stack([stacked(l, "k") for l in L], 1)
    rep["wv"] = np.stack([a[f"L{l}_xcond_Wv"].T for l in L], 1)
    rep["wo"] = np.stack([a[f"L{l}_xcond_Wo"].T for l in L], 1)
    rep["bq"] = np.stack([stacked_bias(l, "q") for l in L], 1)
    rep["bk"] = np.stack([stacked_bias(l, "k") for l in L], 1)
    rep["bv"] = np.stack([rows(a[f"L{l}_xcond_bv"]) for l in L], 1)
    rep["bo"] = np.stack([rows(a[f"L{l}_xcond_bo"]) for l in L], 1)
    rep["u1"] = np.tile(a["L0_ffn_U1"], (1, 4))
    rep["v1"] = np.tile(a["L0_ffn_V1"], (3, 1))
    rep["u2"] = a["L0_ffn_U2"].reshape(FF_BLOCKS, 128, RANK).transpose(1, 0, 2)
    rep["v2"] = np.tile(a["L0_ffn_V2"], (4, 1))
    rep["b1"] = a["L0_ffn_b1"].reshape(FF_BLOCKS, 128).T
    rep["b2"] = rows(a["L0_ffn_b2"])
    rep["gate"] = a["L1_ffn_gate_w"].T
    rep["w1"] = a["L1_ffn_w1"].transpose(1, 0, 2).reshape(128, EXPERTS * FF)
    rep["w2"] = a["L1_ffn_w2"].reshape(EXPERTS * FF_BLOCKS, 128, DIM).transpose(1, 0, 2).reshape(128, -1)
    rep["e_b1"] = a["L1_ffn_b1"].reshape(EXPERTS * FF_BLOCKS, 128).T
    rep["e_b2"] = rows(a["L1_ffn_b2"].reshape(1, -1))
    rep["before"] = np.triu(np.ones((128, 128), np.float32), 1)
    rep["tie"] = rows(np.tril(np.ones((EXPERTS, EXPERTS), np.float32), -1).reshape(1, -1))
    rep["iota"] = np.concatenate([np.arange(BLOCKS), 128 * np.arange(BLOCKS), 8 ** (np.arange(BLOCKS) % UNROLL), 128 * np.arange(16)])[None].astype(np.float32)
    rep["regions"] = rows((REGION * np.arange(EXPERTS))[None].astype(np.float32))
    token = SEQ * np.arange(BATCH)[None, :, None] + TILES * np.arange(128)[:, None, None] + np.arange(TILES)
    rep["ids"] = (TOPK * token[..., None] + np.arange(TOPK)).astype(np.int32).view(np.float32).reshape(128, TOKEN_TILES, TOPK)
    pad = np.zeros(((EXPERTS + SPARE) * 128, ROW), np.int32)
    pad[:, DIM] = TOKENS * TOPK + np.arange(len(pad))
    rep["pad_rows"] = pad.view(np.float32)
    return {k: np.ascontiguousarray(v) for k, v in rep.items()}


def kernel(**inputs):
    import concourse.bacc as bacc
    from concourse.bass_utils import run_bass_kernel_spmd

    nc = bacc.Bacc("TRN2", target_bir_lowering=False, num_devices=1)
    arrays = {f"in_{k}": v for k, v in arrays_for(inputs).items()}
    io = {k[3:]: nc.dram_tensor(k, v.shape, mybir.dt.from_np(v.dtype), kind="ExternalInput").ap() for k, v in arrays.items()}
    out = nc.dram_tensor("out", (BATCH, 128, TILES, DIM), mybir.dt.float32, kind="ExternalOutput").ap()
    pixart_blocks(nc, io, out)
    r = run_bass_kernel_spmd(nc, [arrays], core_ids=[0])
    return r.results[0]["out"].reshape(BATCH, SEQ, DIM)
```

```python
from contextlib import ExitStack

import numpy as np
import concourse.bass as bass
from concourse import mybir

LAYERS, BATCH, SEQ, DIM, CTX = 2, 4, 512, 128, 77
HEADS, HEAD_DIM = 16, 8
GROUPS, PER_GROUP = 4, 4
TILES = SEQ // 128
RANK, FF, FF_BLOCKS = 32, 512, 4
EXPERTS, TOPK = 8, 2
CTX_ALL = BATCH * CTX
ONE_ROWS, MAX_ROW = 2, 98
ROUNDS = LAYERS * BATCH
PROB_SLOTS = 10
RING = 4
NUM_STEP, DEN_STEP = 5, 7
COPY_STEPS = (4, 5)
STATS_STEP, APPLY_STEPS = 0, (7, 8, 9, 10)
FRONT_AT = {step: [("q", step)] for step in range(GROUPS)}
_tiles = [("a", c, t) for c in range(GROUPS) for t in range(TILES)]
for _step, _n in zip(range(3, 13), (1, 2, 2, 1, 2, 2, 1, 2, 2, 1)):
    FRONT_AT[_step] = FRONT_AT.get(_step, []) + [_tiles.pop(0) for _ in range(_n)]
FRONT_AT[13] = [("mt",)]


def front_at(r, step):
    return [w for w in FRONT_AT.get(step, []) if not (r % BATCH == 1 and w in (("q", 0), ("q", 1)))]


def finish_steps(r):
    return ((6, 9, 12, 13), 14, 15) if (r + 1) % BATCH else ((4, 5, 6, 7), 8, 9)


ROUTE_AT = {(6, 1): [("stats", 0)], (6, 3): [("tile 0", 0)], (6, 4): [("tile 1", 0)], (6, 5): [("tile 2", 0)],
            (6, 6): [("tile 3", 0)], (6, 15): [("transpose", 0)],
            (7, 0): [("stats", 1)], (7, 1): [("logits", 0)], (7, 2): [("exp", 0)], (7, 3): [("choose", 0), ("tile 0", 1)],
            (7, 4): [("tile 1", 1)], (7, 5): [("tile 2", 1)], (7, 6): [("count", 0), ("tile 3", 1)],
            (7, 7): [("place", 0)], (7, 8): [("transpose", 1)], (7, 9): [("logits", 1)], (7, 10): [("exp", 1), ("stats", 2)],
            (7, 11): [("choose", 1)], (7, 14): [("count", 1)], (7, 15): [("place", 1)]}
ON_VECTOR = (0, 1, 5, 6, 7, 8, 9)
WARM_BEFORE, WARM_MOE = 6, 14
NORM_ORDER = [*range(7), 8, 7, *range(9, 4 * BATCH)]
QUERY_DMAS, KEY_DMAS, VALUE_DMAS, FFN_DMAS, MOE_DMAS = 3, 2, 4, 6, 10


def maxima_parts(r, warm=0):
    return [item for i in range(3, 13, 2) for item in [("maxima", r, range(i, i + 2))] + [("warm", 1)] * warm]


BEFORE_0 = [("apply", 0), ("tr", 0), ("q", 0, 0), ("k", 0, 0), ("q", 0, 1), ("k", 0, 1), ("q", 0, 2), ("k", 0, 2),
            ("q", 0, 3), ("k", 0, 3), ("spread", 0, 0), ("v", 0, 0), ("stats", 1), *maxima_parts(0, warm=1),
            ("apply", 1), ("front", 0, range(13, HEADS)), ("warm", 1), ("tr", 1), ("warm", 1), ("q", 1, 0), ("q", 1, 1),
            ("spread", 0, 1), ("v", 0, 1)]
BESIDE = {(0, 13): [("spread", 0, 2), ("v", 0, 2)], (0, 14): [("tr", 2)],
          (1, 13): [("spread", 0, 3), ("v", 0, 3)], (1, 14): [("tr", 3)],
          (3, 0): [("stats", 5), ("k", 1, 0)], (3, 1): [("k", 1, 1)], (3, 2): [("k", 1, 2)],
          (3, 3): [("apply", 5), ("k", 1, 3)], (3, 5): [("v", 1, 0)], (3, 6): [("v", 1, 1)],
          (3, 7): [("ftr", 0)], (3, 8): [("fp", 0), ("v", 1, 2)],
          (3, 10): [("stats", 6), ("ftr", 1), ("spread", 1, 0)], (3, 11): [("fp", 1)], (3, 12): [("apply", 6), ("spread", 1, 1)],
          (3, 14): [("ftr", 2), ("spread", 1, 2)], (3, 15): [("fp", 2)], (4, 14): [("tr", 6)], (5, 14): [("tr", 7)]}
BETWEEN = [("copy",), ("hidden", 0), ("invert", 0), ("invert", 1), ("invert", 2), ("invert", 3), ("normalise",),
           ("hidden", 1), ("fq", 0), ("o",), ("fo", 0), ("stats", 8), ("hidden", 2), ("stats", 7), ("fq", 1), ("apply", 8),
           ("tr", 4), ("fo", 1), ("q", 4, 0), ("apply", 7), ("q", 4, 1), ("q", 4, 2), ("ftr", 3), ("q", 4, 3), ("stats", 9),
           *maxima_parts(4)[0:1], ("fp", 3), *maxima_parts(4)[1:2], ("fq", 2), ("hidden", 3), *maxima_parts(4)[2:3], ("fo", 2),
           *maxima_parts(4)[3:4], ("fq", 3), *maxima_parts(4)[4:5], ("fo", 3), ("apply", 9), ("exp table",),
           ("front", 4, range(13, HEADS)), ("warm", 1), ("tr", 5), ("q", 5, 0), ("q", 5, 1), ("v", 1, 3), ("spread", 1, 3)]

TOKENS = BATCH * SEQ
TOKEN_TILES = BATCH * TILES
REGION = TOKENS + 128
ROW = DIM + 2 * EXPERTS
GOES, WEIGHT = DIM, DIM + EXPERTS
BLOCKS = TOKENS * TOPK // 128 + EXPERTS
SPARE = BLOCKS - TOKENS * TOPK // 128
UNROLL = 8
STACK = 96 + ONE_ROWS + HEADS
SCALE = 1.0 / float(np.sqrt(np.float32(HEAD_DIM)))
LN_EPS = 1e-5


def pixart_blocks(nc, io, out):
    f32, f32r = mybir.dt.float32, mybir.dt.float32r
    ACT, ALU, AX = mybir.ActivationFunctionType, mybir.AluOpType, mybir.AxisListType

    with ExitStack() as ctx:
        def sb(name, shape, dt=f32):
            return ctx.enter_context(nc.sbuf_tensor(name, shape, dt))

        def sem(name):
            return ctx.enter_context(nc.semaphore(name))

        ident = sb("ident", [128, 128])
        ctx_t = sb("ctx_t", [128, CTX_ALL])
        wq = sb("wq", [128, LAYERS, GROUPS, 128])
        wk = sb("wk", [128, LAYERS, GROUPS, 128])
        wv = sb("wv", [128, LAYERS, 128])
        wo = sb("wo", [128, LAYERS, 128])
        small = sb("small", [128, 2 * LAYERS * GROUPS + PER_GROUP + BATCH + FF_BLOCKS + 1])
        cuts = np.cumsum([0, LAYERS * GROUPS, LAYERS * GROUPS, PER_GROUP, BATCH, FF_BLOCKS, 1])
        bq, bk, member, tau, b1, low_row = (small[:, int(i):int(j)] for i, j in zip(cuts, cuts[1:]))
        bq, bk = (v.rearrange("p (l c) -> p l c", l=LAYERS) for v in (bq, bk))
        wide = sb("wide", [128, 2 * LAYERS + 1, 128])
        bv, bo, b2 = wide[:, 0:LAYERS], wide[:, LAYERS:2 * LAYERS], wide[:, 2 * LAYERS]
        taus = sb("taus", [128, BATCH])
        bqs = sb("bqs", [128, BATCH, LAYERS, GROUPS])
        delta = sb("delta", [128, CTX_ALL])
        delta_hi = sb("delta_hi", [128, CTX_ALL])
        delta_rows = sb("delta_rows", [128, CTX_ALL], f32r)
        ones_v = sb("ones_v", [128, PER_GROUP, 32])
        zeros = sb("zeros", [128, SEQ])
        x = sb("x", [128, BATCH, TILES, DIM])
        xb = sb("xb", [128, BATCH, TILES, DIM])
        xn = sb("xn", [128, 2, TILES, DIM])
        xt = sb("xt", [128, 2, SEQ])
        ln_stats = sb("ln_stats", [128, 3, TILES, 6])
        ln_mv = sb("ln_mv", [128, 3, TILES, 2])
        ln_var = sb("ln_var", [128, 3, TILES])
        ln_pow = sb("ln_pow", [128, 3, TILES])
        ln_rstd = sb("ln_rstd", [128, 3, TILES])
        ln_scaled = sb("ln_scaled", [128, 3, TILES])
        ln_shift = sb("ln_shift", [128, 3, TILES])
        nothing = sb("nothing", [1, 1])
        minus_half = sb("minus_half", [128, TILES])
        qs = sb("qs", [128, 2, GROUPS, SEQ], f32r)
        ks = sb("ks", [128, BATCH, GROUPS, PER_GROUP, CTX], f32r)
        vm = sb("vm", [128, BATCH, HEADS, 32])
        maxima = sb("maxima", [128, 2, TILES, 128])
        probs = sb("probs", [128, PROB_SLOTS, SEQ])
        sums = sb("sums", [128, 2, SEQ])
        rden = sb("rden", [128, SEQ])
        ot = sb("ot", [128, SEQ])
        u1 = sb("u1", [128, 128])
        v1 = sb("v1", [128, FF])
        v1hi = sb("v1hi", [128, FF])
        v1s = sb("v1s", [128, FF], f32r)
        u2 = sb("u2", [128, FF_BLOCKS, RANK])
        v2 = sb("v2", [128, 128])
        pstack = sb("pstack", [128, 3, SEQ], f32r)
        hid = sb("hid", [128, 2, FF_BLOCKS, SEQ])
        q4 = sb("q4", [128, SEQ])
        kr = sb("kr", [128, GROUPS, CTX_ALL], f32r)

        gate = sb("gate", [128, EXPERTS])
        w1 = sb("w1", [128, EXPERTS * FF])
        w2 = sb("w2", [128, EXPERTS * FF_BLOCKS * DIM])
        e_b1 = sb("e_b1", [128, EXPERTS * FF_BLOCKS])
        e_b2 = sb("e_b2", [128, EXPERTS * DIM])
        before = sb("before", [128, 128])
        all_ones = sb("all_ones", [128, 128])
        tie = sb("tie", [128, EXPERTS * EXPERTS])
        iota = sb("iota", [1, 3 * BLOCKS + 16])
        second_at = sb("second_at", [128, TOKEN_TILES])
        xtm = sb("xtm", [128, SEQ])
        lmax = sb("lmax", [128, TILES])
        logit = sb("logit", [128, TILES, EXPERTS])
        expl = sb("expl", [128, TILES, EXPERTS])
        rsum = sb("rsum", [128, 2, TILES])
        greater = sb("greater", [128, TILES, EXPERTS, EXPERTS])
        equal = sb("equal", [128, TILES, EXPERTS, EXPERTS])
        rank = sb("rank", [128, TILES, EXPERTS])
        chosen = sb("chosen", [128, 2, TOPK + 1, TILES, EXPERTS])
        picked = sb("picked", [128, TILES, EXPERTS])
        offset = sb("offset", [128, TOKEN_TILES + 1, EXPERTS])
        place = sb("place", [128, TILES, EXPERTS])
        slot_f = sb("slot_f", [128, TILES, TOPK])
        slots = sb("slots", [128, TOKEN_TILES, TOPK], mybir.dt.int32)
        counts = sb("counts", [1, EXPERTS])
        blk_cmp = sb("blk_cmp", [1, EXPERTS, 16])
        blk_end = sb("blk_end", [1, EXPERTS])
        ended = sb("ended", [1, BLOCKS, EXPERTS])
        ended_at = sb("ended_at", [1, BLOCKS, EXPERTS])
        blk_f = sb("blk_f", [1, 4, BLOCKS])
        turn_f = sb("turn_f", [1, BLOCKS // UNROLL])
        turn_i = sb("turn_i", [1, BLOCKS // UNROLL], mybir.dt.int32)
        turn_last = sb("turn_last", [1, BLOCKS // UNROLL], mybir.dt.int32)
        turn_experts = sb("turn_experts", [1, BLOCKS // UNROLL], mybir.dt.int32)
        blk_row = sb("blk_row", [1, BLOCKS], mybir.dt.int32)
        pad_at = sb("pad_at", [1, EXPERTS], mybir.dt.int32)
        goes_to = sb("goes_to", [128, UNROLL], mybir.dt.uint32)
        xs = sb("xs", [128, 2, 128])
        spare = hid[:].rearrange("p h i n -> p (h i n)")
        sizes = np.cumsum([0, 2 * TILES * ROW, UNROLL * ROW, 2 * FF])
        xm = spare[:, 0:sizes[1]].rearrange("p (h t r) -> p h t r", h=2, t=TILES)
        rows = spare[:, sizes[1]:sizes[2]].rearrange("p (u r) -> p u r", u=UNROLL)
        zs = spare[:, sizes[2]:sizes[3]].rearrange("p (h f) -> p h f", h=2)
        yt = probs[:, 0:8].rearrange("p (b s) n -> p b (s n)", b=BATCH)
        ht = probs[:, 4:6].rearrange("p h (i n) -> p h i n", i=FF_BLOCKS)
        ys = probs[:, 6:8].rearrange("p s (u d) -> p (s u) d", u=UNROLL // 2)
        sorted_rows = nc.dram_tensor("sorted_rows", [EXPERTS * REGION + SPARE * 128, ROW], f32, kind="Internal").ap()
        results = nc.dram_tensor("results", [TOKENS * TOPK + (EXPERTS + SPARE) * 128, DIM], f32, kind="Internal").ap()

        ring = ctx.enter_context(nc.psum_tensor("ring", [128, RING, 512], f32))
        sc = ctx.enter_context(nc.psum_tensor("sc", [128, 2, 512], f32))
        num_den = ctx.enter_context(nc.psum_tensor("num_den", [128, 2, 512], f32))

        zeros_set = sem("zeros_set")
        query_in = sem("query_in")
        key_in = sem("key_in")
        value_in = sem("value_in")
        delta_in = sem("delta_in")
        x_in = [sem(f"x_in{b}") for b in range(BATCH)]
        ffn_in = sem("ffn_in")
        sel_in = sem("sel_in")
        delta_rep = sem("delta_rep")
        max_rep = sem("max_rep")
        x_out = sem("x_out")
        ones_set = sem("ones_set")
        vm_zero = sem("vm_zero")
        delta_scaled = sem("delta_scaled")
        delta_split = sem("delta_split")
        taus_done = sem("taus_done")
        bqs_done = sem("bqs_done")
        k_high = sem("k_high")
        ks_even = sem("ks_even")
        ks_odd = sem("ks_odd")
        stats_done = sem("stats_done")
        mv_done = sem("mv_done")
        var_done = sem("var_done")
        pow_done = sem("pow_done")
        rstd_done = sem("rstd_done")
        scaled_mean = sem("scaled_mean")
        shift_done = sem("shift_done")
        xm_done = sem("xm_done")
        xn_done = {True: sem("xn_by_vector"), False: sem("xn_by_scalar")}
        q_high = sem("q_high")
        scores_ready = sem("scores_ready")
        exp_done = sem("exp_done")
        num_ready = sem("num_ready")
        den_ready = sem("den_ready")
        num_copied = sem("num_copied")
        den_copied = sem("den_copied")
        rden_done = sem("rden_done")
        ot_done = sem("ot_done")
        xb_done = sem("xb_done")
        v1_split = sem("v1_split")
        p_high = sem("p_high")
        h_ready = sem("h_ready")
        h_done = sem("h_done")
        moe_in = sem("moe_in")
        chain_done = sem("chain_done")
        exp_logit = sem("exp_logit")
        selected = sem("selected")
        placed = sem("placed")
        rows_sent = [sem(f"rows_sent{b}") for b in range(BATCH)]
        pads_sent = sem("pads_sent")
        table_done = sem("table_done")
        rows_in = [sem(f"rows_in{u}") for u in range(UNROLL)]
        x_ready = sem("x_ready")
        xs_done = sem("xs_done")
        z_ready = sem("z_ready")
        zs_done = sem("zs_done")
        zt_ready = sem("zt_ready")
        ht_done = sem("ht_done")
        y_ready = sem("y_ready")
        ys_done = sem("ys_done")
        ys_weighed = sem("ys_weighed")
        pads_known = sem("pads_known")
        ys_sent = [sem(f"ys_sent{u}") for u in range(UNROLL)]
        yt_in = [sem(f"yt_in{b}") for b in range(BATCH)]
        first_added = sem("first_added")
        x_final = sem("x_final")
        ring_full = [sem(f"ring_full{i}") for i in range(RING)]
        ring_drained = [sem(f"ring_drained{i}") for i in range(RING)]

        def front_uses(r, step):
            return [(w[0], r, *w[1:]) for w in front_at(r, step)]

        def norm_after_next(r, step):
            n = BATCH if r == 2 else ln_of_round(r + 2) if r % BATCH + 2 < BATCH else None
            if n is None:
                return []
            return [("stats", n)] if step == STATS_STEP else [("apply", n, APPLY_STEPS.index(step))] if step in APPLY_STEPS else []

        def routing(r, step):
            return ROUTE_AT.get((r, step), [])

        def route_uses(stage, b):
            name = {"transpose": "rt", "logits": "rl", "count": "rc"}.get(stage)
            return [(name, b)] if name else [("o", BATCH + b)] if stage == "output" else []

        B2, B3 = BATCH - 2, BATCH - 1
        LATE = [*(("tile %d" % t, B2) for t in range(TILES)), ("transpose", B2), ("logits", B2), ("exp", B2),
                ("warm", 2), ("output", B3), ("warm", 2), ("stats", B3), ("choose", B2), ("count", B2), ("place", B2),
                *(("tile %d" % t, B3) for t in range(TILES)), ("transpose", B3), ("logits", B3), ("exp", B3),
                ("choose", B3), ("count", B3), ("place", B3)]

        def stage_uses(kind, *which):
            if kind == "maxima":
                r, steps = which
                return [u for step in steps for u in front_uses(r, step) if u[0] == "a"]
            if kind == "front":
                r, steps = which
                return [u for step in steps for u in front_uses(r, step)]
            if kind == "o":
                return [("o", BATCH - 1)]
            return [(kind, *which)] if kind in ("tr", "q", "k", "v", "ftr", "fp", "fq", "fo") else []

        uses = []
        for l in range(LAYERS):
            uses += [u for stage in (BETWEEN if l else BEFORE_0) for u in stage_uses(*stage)]
            for b in range(BATCH):
                r = BATCH * l + b
                for step in range(HEADS):
                    if b + 1 < BATCH:
                        uses += front_uses(r + 1, step)
                    if step == finish_steps(r)[2] and b:
                        uses.append(("o", r - 1))
                    uses += [u for stage, rb in routing(r, step) for u in route_uses(stage, rb)]
                    uses += [u for stage in BESIDE.get((r, step), []) for u in stage_uses(*stage)]
        uses += [u for stage, b in LATE for u in route_uses(stage, b)]
        at = {u: i for i, u in enumerate(uses)}

        def bank(*u):
            return ring[:, at[u] % RING, :]

        def wait_full(eng, *u):
            eng.wait_ge(ring_full[at[u] % RING], at[u] // RING + 1)

        def wait_drained(eng, *u):
            eng.wait_ge(ring_drained[at[u] % RING], at[u] // RING + 1)

        def wait_bank(eng, *u):
            if at[u] >= RING:
                eng.wait_ge(ring_drained[at[u] % RING], at[u] // RING)

        def fills(ins, *u):
            ins.then_inc(ring_full[at[u] % RING], 1)

        def drains(ins, *u):
            ins.then_inc(ring_drained[at[u] % RING], 1)

        def hbank(i):
            return sc[:, i] if i < 2 else num_den[:, i - 2]

        def ln_of_round(r):
            return r if r < BATCH else r + BATCH

        def wait_x(eng, n):
            kind, b = n // BATCH, n % BATCH
            if kind == 0:
                eng.wait_ge(x_in[b], 16)
            elif kind == 1:
                wait_drained(eng, "o", b)
            elif kind == 2:
                wait_drained(eng, "fo", b)
            else:
                wait_drained(eng, "o", BATCH + b)

        def nth(n):
            return NORM_ORDER.index(n) + 1

        def norms_of(vector, n):
            return sum((i in ON_VECTOR) == vector for i in NORM_ORDER[:nth(n)])

        def wait_xn(eng, n):
            eng.wait_ge(xn_done[n in ON_VECTOR], norms_of(n in ON_VECTOR, n))

        def reader_of(n):
            return None if n < 2 else ("tr", n - 2) if n < 6 else ("ftr", n - 6) if n < 10 else ("tr", n - 6)

        def ln_slot(n):
            return n % 2 if n < 3 * BATCH else 2

        def wait(eng, semaphore, value):
            if not isinstance(value, int) or value > 0:
                eng.wait_ge(semaphore, value)

        def experts_of(eng, turn):
            packed = eng.value_load(turn_experts[0:1, bass.ds(turn, 1)], min_val=0, max_val=(1 << 3 * UNROLL + 6) - 1)
            return {u: (packed >> 3 * (u % (UNROLL + 2))) & (EXPERTS - 1) for u in range(-2, UNROLL)}

        def keys_of(b):
            return kr[0:96, :, b * CTX:(b + 1) * CTX].bitcast(f32)

        def pad_experts(eng, experts):
            eng.wait_ge(pads_known, 1)
            for e in experts:
                at_row = eng.value_load(pad_at[0:1, e:e + 1], min_val=0, max_val=(EXPERTS - 1) * REGION + TOKENS)
                eng.dma_start(sorted_rows[bass.ds(at_row, 128), :], io["pad_rows"][128 * e:128 * e + 128]).then_inc(pads_sent, 16)

        TURNS = BLOCKS // UNROLL

        block = ctx.enter_context(nc.Block())

        @block.sync
        def _(sp):
            sp.dma_start(x[:, 0], io["x"][0]).then_inc(x_in[0], 16)
            sp.dma_start(small[:], io["small"]).then_inc(query_in, 16)
            sp.dma_start(wq[:, 0], io["wq"][:, 0]).then_inc(query_in, 16)
            sp.dma_start(delta[96:98, :], io["delta"].to_broadcast([2, CTX_ALL])).then_inc(delta_in, 16)
            sp.dma_start(x[:, 1], io["x"][1]).then_inc(x_in[1], 16)
            sp.dma_start(ones_v[:], io["ones_v"]).then_inc(value_in, 16)
            sp.dma_start(wv[:], io["wv"]).then_inc(value_in, 16)
            sp.dma_start(wide[:], io["wide"]).then_inc(value_in, 16)
            sp.dma_start(wo[:], io["wo"]).then_inc(value_in, 16)
            for b in range(2, BATCH):
                sp.dma_start(x[:, b], io["x"][b]).then_inc(x_in[b], 16)
            sp.wait_ge(delta_split, 2)
            for b in range(BATCH):
                src = delta_rows[96:98, b * CTX:(b + 1) * CTX].bitcast(f32).unsqueeze(1).to_broadcast([2, HEADS, CTX])
                sp.dma_start(ks[96:98, b].bitcast(f32).rearrange("p c j k -> p (c j) k"), src).then_inc(delta_rep, 16)
            sp.dma_start(wk[:, 1], io["wk"][:, 1]).then_inc(ffn_in, 16)
            sp.dma_start(wq[:, 1], io["wq"][:, 1]).then_inc(ffn_in, 16)
            sp.dma_start(u1[:], io["u1"]).then_inc(ffn_in, 16)
            sp.dma_start(v1[0:96, :], io["v1"]).then_inc(ffn_in, 16)
            sp.dma_start(u2[:], io["u2"]).then_inc(ffn_in, 16)
            sp.dma_start(v2[:], io["v2"]).then_inc(ffn_in, 16)
            sp.dma_start(offset[:, 0], io["regions"]).then_inc(moe_in, 16)
            for name, tile in (("gate", gate), ("before", before), ("tie", tie), ("iota", iota), ("e_b1", e_b1),
                               ("e_b2", e_b2), ("w1", w1), ("w2", w2), ("second_at", second_at)):
                sp.dma_start(tile[:], io[name]).then_inc(moe_in, 16)
            sp.dma_start(sorted_rows[EXPERTS * REGION:, :], io["pad_rows"][EXPERTS * 128:]).then_inc(pads_sent, 16)
            for r in range(ROUNDS):
                wait_drained(sp, "mt", r)
                src = qs[96:128, r % 2, 0, :].bitcast(f32).unsqueeze(1).to_broadcast([32, GROUPS - 1, SEQ])
                sp.dma_start(qs[96:128, r % 2, 1:GROUPS, :].bitcast(f32), src).then_inc(max_rep, 16)
            pad_experts(sp, range(0, EXPERTS, 2))
            sp.wait_ge(pads_sent, 16 * (EXPERTS + 1))
            for b in range(BATCH):
                sp.wait_ge(rows_sent[b], 16 * TILES * TOPK)
            sp.wait_ge(table_done, 1)

            def load_blocks(turn):
                for u in range(UNROLL):
                    n = turn * UNROLL + u
                    first = sp.value_load(blk_row[0:1, bass.ds(n, 1)], min_val=0, max_val=EXPERTS * REGION + (SPARE - 1) * 128)
                    wait(sp, ys_weighed, n - UNROLL + 1)
                    sp.dma_start(rows[:, u], sorted_rows[bass.ds(first, 128), :]).then_inc(rows_in[u], 16)

            load_blocks(0)
            with sp.Fori(1, TURNS) as turn:
                load_blocks(turn)
            for u in range(UNROLL):
                sp.wait_ge(ys_sent[u], 16 * TURNS)
            for b in range(BATCH):
                src = results[2 * SEQ * b:2 * SEQ * (b + 1), :].rearrange("(p m) d -> p (m d)", p=128)
                sp.dma_start(yt[:, b], src).then_inc(yt_in[b], 16)
            for b in range(BATCH):
                sp.wait_ge(x_final, b + 1)
                sp.dma_start(out[b], x[:, b]).then_inc(x_out, 16)
            sp.wait_ge(x_out, 16 * BATCH)

        @block.gpsimd
        def _(pool):
            pool.dma_start(ks[98:114], io["minus_sel"]).then_inc(sel_in, 16)
            nc.gpsimd.memset(minus_half[:], -0.5).then_inc(ones_set, 1)
            pool.wait_ge(ones_set, 1)

            def fill():
                nc.gpsimd.memset(all_ones[:], 1.0).then_inc(ones_set, 1)
                pool.wait_ge(ones_set, 2)
                nc.gpsimd.memset(qs[96:128, 0].bitcast(f32), 1.0).then_inc(ones_set, 1)
                nc.gpsimd.memset(qs[96:128, 1].bitcast(f32), 1.0).then_inc(ones_set, 1)
                pool.wait_ge(ones_set, 4)
                nc.gpsimd.memset(maxima[:, :, :, 96:98], 1.0).then_inc(ones_set, 1)
                nc.gpsimd.memset(maxima[:, :, :, 0:96], 0.0).then_inc(ones_set, 1)
                nc.gpsimd.memset(maxima[:, :, :, 98:128], 0.0).then_inc(ones_set, 1)
                nc.gpsimd.memset(vm[:], 0.0).then_inc(vm_zero, 1)
                pool.wait_ge(ones_set, 7)
                pool.wait_ge(vm_zero, 1)
                nc.gpsimd.memset(probs[64:128], 0.0).then_inc(ones_set, 1)
                pool.wait_ge(ones_set, 8)

            def scatter_rows(b):
                pool.wait_ge(placed, b + 1)
                for t in range(TILES):
                    for k in range(TOPK):
                        to = slots[:, TILES * b + t, k:k + 1].bitcast(mybir.dt.uint32)
                        pool.indirect_dma_start(out=sorted_rows, out_offset=bass.IndirectOffsetOnAxis(ap=to, axis=0),
                                                in_=xm[:, b % 2, t], in_offset=None).then_inc(rows_sent[b], 16)

            for n in NORM_ORDER:
                s, b = ln_slot(n), n % BATCH
                pool.wait_ge(mv_done, nth(n))
                nc.gpsimd.tensor_scalar(ln_var[:, s], ln_mv[:, s, :, 1], LN_EPS, None, ALU.add).then_inc(var_done, 1)
                pool.wait_ge(var_done, nth(n))
                if n // BATCH in (0, 2):
                    nc.gpsimd.tensor_tensor(ln_pow[:, s], ln_var[:, s], minus_half[:], ALU.pow).then_inc(pow_done, 1)
                    pool.wait_ge(pow_done, (n if n < BATCH else n - BATCH) + 1)
                    if n == 0:
                        pool.wait_ge(taus_done, 1)
                    nc.gpsimd.tensor_scalar(ln_rstd[:, s], ln_pow[:, s], taus[:, b:b + 1], None, ALU.mult).then_inc(rstd_done, 1)
                else:
                    nc.gpsimd.tensor_tensor(ln_rstd[:, s], ln_var[:, s], minus_half[:], ALU.pow).then_inc(rstd_done, 1)
                if n not in ON_VECTOR:
                    i = norms_of(False, n)
                    pool.wait_ge(rstd_done, nth(n))
                    nc.gpsimd.tensor_tensor(ln_scaled[:, s], ln_mv[:, s, :, 0], ln_rstd[:, s], ALU.mult).then_inc(scaled_mean, 1)
                    pool.wait_ge(scaled_mean, i)
                    if n > 3 * BATCH:
                        pool.wait_ge(xm_done, b)
                    nc.gpsimd.tensor_scalar(ln_shift[:, s], ln_scaled[:, s], -1.0, None, ALU.mult).then_inc(shift_done, 1)
                if n == 0:
                    fill()
                if n < 3 * BATCH:
                    if n == 0:
                        pool.wait_ge(value_in, 16 * VALUE_DMAS)
                    wait_x(pool, n)
                    bias = b2 if n // BATCH == 1 else bo[:, n // (2 * BATCH), :]
                    nc.gpsimd.tensor_tensor(xb[:, b], x[:, b], bias.unsqueeze(1).to_broadcast([128, TILES, DIM]),
                                            ALU.add).then_inc(xb_done, 1)
                if n >= 3 * BATCH:
                    if b:
                        scatter_rows(b - 1)
            scatter_rows(BATCH - 1)

            for n in range(BLOCKS):
                u = n % UNROLL
                pool.wait_ge(ys_weighed, n + 1)
                pool.indirect_dma_start(out=results, out_offset=bass.IndirectOffsetOnAxis(ap=goes_to[:, u:u + 1], axis=0),
                                        in_=ys[:, u], in_offset=None).then_inc(ys_sent[u], 16)

        @block.scalar
        def _(act):
            def front(r, step):
                for what, *which in front_at(r, step):
                    front_part(r, what, *which)

            def front_part(r, what, *which):
                s, l, b = r % 2, r // BATCH, r % BATCH
                if what == "q":
                    c, = which
                    wait_full(act, "q", r, c)
                    if r == 0 and c == 0:
                        act.wait_ge(bqs_done, 1)
                    nc.scalar.activation(qs[0:96, s, c], bank("q", r, c)[0:96], ACT.Identity,
                                         bias=bqs[0:96, r % BATCH, l, c:c + 1]).then_inc(q_high, 1)
                elif what == "mt":
                    wait_full(act, "mt", r)
                    if r == 0:
                        act.wait_ge(ones_set, 4)
                    drains(nc.scalar.activation(qs[96:128, s, 0], bank("mt", r)[96:128], ACT.Identity), "mt", r)

            def copy_sums(r, i):
                act.wait_ge(num_ready, r + 1) if i == 0 else act.wait_ge(den_ready, PER_GROUP * (r + 1))
                if r:
                    act.wait_ge(ot_done, r)
                nc.scalar.activation(sums[:, i], num_den[:, i], ACT.Identity).then_inc((num_copied, den_copied)[i], 1)

            def stage(kind, *which):
                if kind == "front":
                    for step in which[1]:
                        front(which[0], step)
                elif kind == "maxima":
                    for step in which[1]:
                        for w in front_at(which[0], step):
                            if w[0] == "a":
                                front_part(which[0], *w)
                elif kind == "q":
                    front_part(which[0], "q", which[1])
                elif kind == "copy":
                    copy_sums(BATCH - 1, 0)
                    copy_sums(BATCH - 1, 1)
                elif kind == "apply" and which[0] not in ON_VECTOR:
                    n, t = which
                    s, b = ln_slot(n), n % BATCH
                    act.wait_ge(shift_done, norms_of(False, n))
                    wait_full(act, *reader_of(n))
                    ins = nc.scalar.activation(xn[:, s, t], x[:, b, t], ACT.Identity,
                                               bias=ln_shift[:, s, t:t + 1], scale=ln_rstd[:, s, t:t + 1])
                    if t == TILES - 1:
                        ins.then_inc(xn_done[False], 1)
                elif kind == "tr":
                    r, = which
                    wait_full(act, "tr", r)
                    drains(nc.scalar.activation(xt[:, r % 2], bank("tr", r), ACT.Identity), "tr", r)
                elif kind == "exp table":
                    nc.scalar.activation(nothing[:], minus_half[0:1, 0:1], ACT.Exp)
                elif kind == "k":
                    l, c = which
                    wait_full(act, "k", l, c)
                    if l and c == 0:
                        act.wait_ge(ks_even, BATCH)
                    nc.scalar.activation(kr[0:96, c], bank("k", l, c)[0:96, 0:CTX_ALL], ACT.Identity,
                                         bias=bk[0:96, l, c:c + 1]).then_inc(k_high, 1)
                elif kind == "spread":
                    l, b = which
                    wait_drained(act, "k", l, GROUPS - 1)
                    for j in (2, 3):
                        ins = nc.scalar.activation(ks[0:96, b, :, j], keys_of(b), ACT.Identity, scale=member[0:96, j:j + 1])
                    ins.then_inc(ks_odd, 1)
                elif kind == "ftr":
                    b, = which
                    wait_full(act, "ftr", b)
                    drains(nc.scalar.activation(xt[:, b % 2], bank("ftr", b), ACT.Identity), "ftr", b)
                elif kind == "fp":
                    b, = which
                    wait_full(act, "fp", b)
                    if b >= 3:
                        act.wait_ge(h_ready, FF_BLOCKS * (b - 2))
                    nc.scalar.activation(pstack[0:96, b % 3], bank("fp", b)[0:96], ACT.Identity).then_inc(p_high, 1)
                elif kind == "hidden":
                    b, = which
                    for i in range(FF_BLOCKS):
                        act.wait_ge(h_ready, FF_BLOCKS * b + i + 1)
                        if b >= 2 and i == 0:
                            wait_full(act, "fq", b - 2)
                        nc.scalar.activation(hid[:, b % 2, i], hbank(i), ACT.Gelu_apprx_tanh,
                                             bias=b1[:, i:i + 1]).then_inc(h_done, 1)

            def route(stage, b):
                if stage.startswith("tile"):
                    t = int(stage[-1])
                    act.wait_ge(shift_done, norms_of(False, 3 * BATCH + b))
                    if b == 0:
                        wait_full(act, "fq", BATCH - 1)
                    if b >= 2:
                        act.wait_ge(rows_sent[b - 2], 16 * TILES * TOPK)
                        wait_full(act, "rt", b - 2)
                    ins = nc.scalar.activation(xm[:, b % 2, t, 0:DIM], x[:, b, t], ACT.Identity,
                                               bias=ln_shift[:, 2, t:t + 1], scale=ln_rstd[:, 2, t:t + 1])
                    if t == TILES - 1:
                        ins.then_inc(xm_done, 1)
                elif stage == "transpose":
                    wait_full(act, "rt", b)
                    drains(nc.scalar.activation(xtm[:], bank("rt", b), ACT.Identity), "rt", b)
                elif stage == "exp":
                    wait_drained(act, "rl", b)
                    nc.scalar.activation(expl[:], logit[:], ACT.Exp).then_inc(exp_logit, 1)

            def weigh(n, u, e):
                act.wait_ge(ys_done, n + 1)
                nc.scalar.activation(ys[:, u], ys[:, u], ACT.Identity,
                                     scale=rows[:, u, bass.ds(e + WEIGHT, 1)]).then_inc(ys_weighed, 1)

            def hidden_blocks(turn, first=False):
                e = experts_of(act, turn)
                for u in range(UNROLL):
                    n = turn * UNROLL + u
                    act.wait_ge(zt_ready, n + 1)
                    wait(act, y_ready, n - 1)
                    for i in range(FF_BLOCKS):
                        ins = nc.scalar.activation(ht[:, u % 2, i], num_den[:, u % 2, 128 * i:128 * i + 128], ACT.Relu,
                                                   bias=e_b1[:, bass.ds(e[u] * FF_BLOCKS + i, 1)])
                    ins.then_inc(ht_done, 1)
                    if not (first and u < 2):
                        weigh(n - 2, (u - 2) % UNROLL, e[u - 2])
                return e

            act.dma_start(ident[:], io["ident"]).then_inc(query_in, 16)
            act.dma_start(ctx_t[:], io["ctx_t"]).then_inc(key_in, 16)
            act.dma_start(wk[:, 0], io["wk"][:, 0]).then_inc(key_in, 16)
            act.wait_ge(ones_set, 1)
            stage("exp table")
            act.wait_ge(query_in, 16 * QUERY_DMAS)
            for l in range(LAYERS):
                for item in BETWEEN if l else BEFORE_0:
                    stage(*item)
                for b in range(BATCH):
                    r = BATCH * l + b
                    for step in range(HEADS):
                        g = HEADS * r + step
                        act.wait_ge(scores_ready, g + 1)
                        if g == 0:
                            act.wait_ge(ones_set, 8)
                        if g >= PROB_SLOTS:
                            last = g - PROB_SLOTS
                            act.wait_ge(den_ready, last // GROUPS + 1)
                        nc.scalar.activation(probs[0:CTX, g % PROB_SLOTS], sc[0:CTX, g % 2], ACT.Exp).then_inc(exp_done, 1)
                        if b and step in COPY_STEPS:
                            copy_sums(r - 1, COPY_STEPS.index(step))
                        if b + 1 < BATCH:
                            front(r + 1, step)
                        for name, rb in routing(r, step):
                            route(name, rb)
                        for item in norm_after_next(r, step):
                            stage(*item)
                        for item in BESIDE.get((r, step), []):
                            stage(*item)
            for name, b in LATE:
                route(name, b)
            pad_experts(act, range(1, EXPERTS, 2))
            act.wait_ge(table_done, 1)
            hidden_blocks(0, first=True)
            with act.Fori(1, TURNS - 1) as turn:
                hidden_blocks(turn)
            e = hidden_blocks(TURNS - 1)
            for u in (UNROLL - 2, UNROLL - 1):
                weigh(BLOCKS - UNROLL + u, u, e[u])

        @block.vector
        def _(dve):
            def ln_stats_of(n):
                s, b = ln_slot(n), n % BATCH
                wait_x(dve, n)
                for t in range(TILES):
                    nc.vector.bn_stats(ln_stats[:, s, t], x[:, b, t]).then_inc(stats_done, 1)
                for t in range(TILES):
                    dve.wait_ge(stats_done, TILES * (nth(n) - 1) + t + 1)
                    ins = nc.vector.bn_aggr(ln_mv[:, s, t], ln_stats[:, s, t])
                ins.then_inc(mv_done, 1)

            def ln_apply(n):
                s, b = ln_slot(n), n % BATCH
                dve.wait_ge(rstd_done, nth(n))
                if reader_of(n):
                    wait_full(dve, *reader_of(n))
                for t in range(TILES):
                    ins = nc.vector.tensor_scalar(xn[:, s, t], x[:, b, t], ln_mv[:, s, t, 0:1], ln_rstd[:, s, t:t + 1],
                                                  ALU.subtract, ALU.mult)
                ins.then_inc(xn_done[True], 1)

            def front(r, step):
                for what, *which in front_at(r, step):
                    front_part(r, what, *which)

            def front_part(r, what, *which):
                s, l, b = r % 2, r // BATCH, r % BATCH
                if what == "q":
                    c, = which
                    dve.wait_ge(q_high, GROUPS * r + c + 1)
                    drains(nc.vector.scalar_tensor_tensor(
                        out=qs[64:96, s, c], in0=bank("q", r, c)[64:96], scalar=bqs[64:96, r % BATCH, l, c:c + 1],
                        in1=qs[64:96, s, c].bitcast(f32), op0=ALU.add, op1=ALU.subtract), "q", r, c)
                elif what == "a":
                    c, t = which
                    if r == 0 and t == 0 and c == 0:
                        dve.wait_ge(ones_set, 7)
                    if r >= 2 and t == 0 and c == 0:
                        wait_full(dve, "mt", r - 2)
                    wait_full(dve, "a", r, c, t)
                    src = bank("a", r, c, t)[:, 0:PER_GROUP * CTX].rearrange("p (j k) -> p j k", k=CTX)
                    col = MAX_ROW + PER_GROUP * c
                    drains(nc.vector.tensor_reduce(maxima[:, s, t, col:col + PER_GROUP], src, AX.X, ALU.max),
                           "a", r, c, t)

            def invert(r, quarter):
                if quarter == 0:
                    dve.wait_ge(den_ready, PER_GROUP * ROUNDS) if r == ROUNDS - 1 else dve.wait_ge(den_copied, r + 1)
                    if r:
                        dve.wait_ge(ot_done, r)
                part = slice(128 * quarter, 128 * quarter + 128)
                nc.vector.reciprocal(rden[:, part], (num_den if r == ROUNDS - 1 else sums)[:, 1, part]).then_inc(rden_done, 1)

            def normalise(r):
                dve.wait_ge(rden_done, 4 * (r + 1))
                dve.wait_ge(num_ready, ROUNDS) if r == ROUNDS - 1 else dve.wait_ge(num_copied, r + 1)
                nc.vector.tensor_tensor(ot[:], (num_den if r == ROUNDS - 1 else sums)[:, 0], rden[:], ALU.mult).then_inc(ot_done, 1)

            def residual(r):
                dve.wait_ge(xb_done, nth(ln_of_round(r)))
                wait_full(dve, "o", r)
                b = r % BATCH
                drains(nc.vector.tensor_tensor(x[:, b].rearrange("p t d -> p (t d)"), bank("o", r),
                                               xb[:, b].rearrange("p t d -> p (t d)"), ALU.add), "o", r)

            def ffn_weights():
                dve.wait_ge(ffn_in, 16 * FFN_DMAS)
                nc.vector.tensor_copy(v1hi[0:96].bitcast(f32r), v1[0:96]).then_inc(v1_split, 1)
                nc.vector.tensor_copy(v1s[0:96], v1[0:96]).then_inc(v1_split, 1)
                dve.wait_ge(v1_split, 2)
                nc.vector.tensor_tensor(v1s[32:64], v1[32:64], v1hi[32:64], ALU.subtract).then_inc(v1_split, 1)

            def stage(kind, *which):
                if kind == "front":
                    for step in which[1]:
                        front(which[0], step)
                elif kind == "maxima":
                    for step in which[1]:
                        for w in front_at(which[0], step):
                            if w[0] == "a":
                                front_part(which[0], *w)
                elif kind == "q":
                    front_part(which[0], "q", which[1])
                elif kind == "stats":
                    ln_stats_of(*which)
                elif kind == "apply":
                    if which[0] in ON_VECTOR:
                        ln_apply(*which)
                elif kind == "k":
                    l, c = which
                    dve.wait_ge(k_high, GROUPS * l + c + 1)
                    if l and c == 0:
                        dve.wait_ge(ks_odd, BATCH)
                    drains(nc.vector.scalar_tensor_tensor(
                        out=kr[32:64, c], in0=bank("k", l, c)[32:64, 0:CTX_ALL], scalar=bk[32:64, l, c:c + 1],
                        in1=kr[32:64, c].bitcast(f32), op0=ALU.add, op1=ALU.subtract), "k", l, c)
                elif kind == "spread":
                    l, b = which
                    wait_drained(dve, "k", l, GROUPS - 1)
                    if l:
                        dve.wait_ge(scores_ready, HEADS * (b + 1))
                    for j in (0, 1):
                        ins = nc.vector.tensor_scalar(ks[0:96, b, :, j], keys_of(b), member[0:96, j:j + 1], None, ALU.mult)
                    ins.then_inc(ks_even, 1)
                elif kind == "v":
                    l, b = which
                    if l:
                        dve.wait_ge(den_ready, PER_GROUP * (b + 1))
                    elif b == 0:
                        dve.wait_ge(vm_zero, 1)
                    wait_full(dve, "v", l, b)
                    for j in range(PER_GROUP):
                        o = vm[0:CTX, b, j::PER_GROUP, 8 * j:8 * j + 8]
                        i0 = bank("v", l, b)[0:CTX, 0:128].rearrange("p (c j d) -> p c j d", c=GROUPS, j=PER_GROUP)[:, :, j]
                        i1 = bv[0:CTX, l].rearrange("p (c j d) -> p c j d", c=GROUPS, j=PER_GROUP)[:, :, j]
                        ins = nc.vector.tensor_tensor(o, i0, i1, ALU.add)
                    drains(ins, "v", l, b)
                elif kind == "invert":
                    invert(BATCH - 1, *which)
                elif kind == "normalise":
                    normalise(BATCH - 1)
                elif kind == "o":
                    residual(BATCH - 1)
                elif kind == "fp":
                    b, = which
                    dve.wait_ge(p_high, b + 1)
                    drains(nc.vector.tensor_tensor(pstack[64:96, b % 3], bank("fp", b)[64:96],
                                                   pstack[64:96, b % 3].bitcast(f32), ALU.subtract), "fp", b)
                elif kind == "fq":
                    b, = which
                    wait_full(dve, "fq", b)
                    drains(nc.vector.tensor_copy(q4[:], bank("fq", b)), "fq", b)
                elif kind == "fo":
                    b, = which
                    dve.wait_ge(xb_done, nth(BATCH + b))
                    wait_full(dve, "fo", b)
                    drains(nc.vector.tensor_tensor(x[:, b].rearrange("p t d -> p (t d)"), bank("fo", b),
                                                   xb[:, b].rearrange("p t d -> p (t d)"), ALU.add), "fo", b)

            chain = [0]

            def chained(ins):
                chain[0] += 1
                ins.then_inc(chain_done, 1)
                dve.wait_ge(chain_done, chain[0])

            def route(stage, b):
                V = nc.vector
                prob = xm[:, b % 2, :, WEIGHT:WEIGHT + EXPERTS]
                tiles = slice(TILES * b, TILES * b + TILES)
                over = lambda ap: ap.unsqueeze(2).to_broadcast([128, TILES, EXPERTS])
                if stage == "stats":
                    ln_stats_of(3 * BATCH + b)
                elif stage == "logits":
                    wait_full(dve, "rl", b)
                    lg = bank("rl", b)[:, 0:TILES * EXPERTS].rearrange("p (t e) -> p t e", t=TILES)
                    chained(V.tensor_reduce(lmax[:], lg, AX.X, ALU.max))
                    drains(V.tensor_tensor(logit[:], lg, over(lmax[:]), ALU.subtract), "rl", b)
                elif stage == "choose":
                    dve.wait_ge(exp_logit, b + 1)
                    if b >= 2:
                        dve.wait_ge(rows_sent[b - 2], 16 * TILES * TOPK)
                    chained(V.tensor_reduce(rsum[:, 0], expl[:], AX.X, ALU.add))
                    chained(V.reciprocal(rsum[:, 1], rsum[:, 0]))
                    chained(V.tensor_tensor(prob, expl[:], over(rsum[:, 1]), ALU.mult))
                    own = prob.unsqueeze(3).to_broadcast([128, TILES, EXPERTS, EXPERTS])
                    other = prob.unsqueeze(2).to_broadcast([128, TILES, EXPERTS, EXPERTS])
                    V.tensor_tensor(greater[:], other, own, ALU.is_gt)
                    chained(V.tensor_tensor(equal[:], other, own, ALU.is_equal))
                    flat = lambda t: t[:].rearrange("p t a b -> p t (a b)")
                    chained(V.tensor_tensor(flat(equal), flat(equal),
                                            tie[:].unsqueeze(1).to_broadcast([128, TILES, EXPERTS * EXPERTS]), ALU.mult))
                    chained(V.tensor_tensor(flat(greater), flat(greater), flat(equal), ALU.add))
                    chained(V.tensor_reduce(rank[:], greater[:], AX.X, ALU.add))
                    if b >= 2:
                        wait_drained(dve, "rc", b - 2)
                    for k in range(TOPK):
                        V.tensor_scalar(chosen[:, b % 2, k], rank[:], float(k), None, ALU.is_equal)
                    V.tensor_scalar(chosen[:, b % 2, TOPK], rank[:], float(TOPK), None, ALU.is_lt).then_inc(selected, 1)
                    dve.wait_ge(selected, b + 1)
                    V.tensor_tensor(xm[:, b % 2, :, GOES:GOES + EXPERTS],
                                    second_at[:, tiles].unsqueeze(2).to_broadcast([128, TILES, EXPERTS]),
                                    chosen[:, b % 2, 0], ALU.subtract)
                elif stage == "place":
                    wait_full(dve, "rc", b)
                    cnt = bank("rc", b)
                    totals = cnt[:, TILES * EXPERTS:2 * TILES * EXPERTS].rearrange("p (t e) -> p t e", t=TILES)
                    for t in range(TILES):
                        i = TILES * b + t
                        chained(V.tensor_tensor(offset[:, i + 1], totals[:, t], offset[:, i], ALU.add))
                    drains(V.tensor_tensor(place[:], cnt[:, 0:TILES * EXPERTS].rearrange("p (t e) -> p t e", t=TILES),
                                           offset[:, tiles], ALU.add), "rc", b)
                    wait_drained(dve, "rc", b)
                    for k in range(TOPK):
                        chained(V.tensor_tensor(picked[:], chosen[:, b % 2, k], place[:], ALU.mult))
                        chained(V.tensor_reduce(slot_f[:, :, k], picked[:], AX.X, ALU.add))
                    V.tensor_copy(slots[:, tiles], slot_f[:]).then_inc(placed, 1)

            def block_table():
                V = nc.vector
                last = offset[0:1, TOKEN_TILES]
                block_no, block_row, digit = (iota[:, i * BLOCKS:(i + 1) * BLOCKS] for i in range(3))
                whole = iota[:, 3 * BLOCKS:]
                V.tensor_copy(pad_at[:], last).then_inc(pads_known, 1)
                chained(V.tensor_tensor(counts[:], last, offset[0:1, 0], ALU.subtract))
                chained(V.tensor_tensor(blk_cmp[:], counts[:].unsqueeze(2).to_broadcast([1, EXPERTS, 16]),
                                        whole.unsqueeze(1).to_broadcast([1, EXPERTS, 16]), ALU.is_gt))
                chained(V.tensor_reduce(blk_end[:], blk_cmp[:], AX.X, ALU.add))
                for e in range(1, EXPERTS):
                    chained(V.tensor_tensor(blk_end[:, e:e + 1], blk_end[:, e:e + 1], blk_end[:, e - 1:e], ALU.add))
                ends = blk_end[:].unsqueeze(1).to_broadcast([1, BLOCKS, EXPERTS])
                chained(V.tensor_tensor(ended[:], block_no.unsqueeze(2).to_broadcast([1, BLOCKS, EXPERTS]), ends, ALU.is_ge))
                chained(V.tensor_tensor(ended_at[:], ended[:], ends, ALU.mult))
                V.tensor_reduce(blk_f[:, 0], ended[:], AX.X, ALU.add)
                chained(V.tensor_reduce(blk_f[:, 1], ended_at[:], AX.X, ALU.max))
                V.tensor_scalar(blk_f[:, 2], blk_f[:, 0], float(EXPERTS - 1), None, ALU.min)
                chained(V.scalar_tensor_tensor(out=blk_f[:, 3], in0=blk_f[:, 1], scalar=-128.0, in1=block_row,
                                               op0=ALU.mult, op1=ALU.add))
                chained(V.scalar_tensor_tensor(out=blk_f[:, 1], in0=blk_f[:, 0], scalar=float(REGION), in1=blk_f[:, 3],
                                               op0=ALU.mult, op1=ALU.add))
                chained(V.tensor_tensor(blk_f[:, 2], blk_f[:, 2], digit, ALU.mult))
                chained(V.tensor_reduce(turn_f[:], blk_f[:, 2].rearrange("p (t u) -> p t u", u=UNROLL), AX.X, ALU.add))
                chained(V.tensor_copy(turn_i[:], turn_f[:]))
                V.tensor_copy(turn_experts[:, 0:1], turn_i[:, 0:1])
                chained(V.tensor_scalar(turn_last[:, 1:], turn_i[:, :-1], 3 * (UNROLL - 2), 3 * UNROLL,
                                        ALU.logical_shift_right, ALU.logical_shift_left))
                chained(V.tensor_tensor(turn_experts[:, 1:], turn_i[:, 1:], turn_last[:, 1:], ALU.bitwise_or))
                V.tensor_copy(blk_row[:], blk_f[:, 1]).then_inc(table_done, 1)

            def take_up(n, u):
                dve.wait_ge(x_ready, n + 1)
                wait(dve, z_ready, n - 1)
                nc.vector.tensor_copy(xs[:, u % 2], ring[:, u % 2, 0:128]).then_inc(xs_done, 1)

            def evacuate(n, u):
                dve.wait_ge(z_ready, n + 1)
                wait(dve, zt_ready, n - 1)
                nc.vector.tensor_copy(zs[:, u % 2], ring[:, 2 + u % 2]).then_inc(zs_done, 1)

            def finish(n, u, e, turn):
                wait(dve, ys_sent[u], 16 * turn)
                dve.wait_ge(y_ready, n + 1)
                nc.vector.tensor_copy(goes_to[:, u:u + 1], rows[:, u, bass.ds(e + GOES, 1)])
                nc.vector.tensor_tensor(ys[:, u], sc[:, u % 2, 0:DIM], e_b2[:, bass.ds(e * DIM, DIM)],
                                        ALU.add).then_inc(ys_done, 1)

            def moe_blocks(turn, first=False, last=False):
                n0 = turn * UNROLL
                e = experts_of(dve, turn)
                for u in range(UNROLL):
                    if not (last and u == UNROLL - 1):
                        take_up(n0 + u + 1, (u + 1) % UNROLL)
                    evacuate(n0 + u, u)
                    if not (first and u < 2):
                        finish(n0 + u - 2, (u - 2) % UNROLL, e[u - 2], turn + (u - 2) // UNROLL)
                return e

            nc.vector.memset(zeros[:], 0.0).then_inc(zeros_set, 1)
            stage("stats", 0)
            dve.wait_ge(query_in, 16 * QUERY_DMAS)
            nc.vector.tensor_scalar(taus[:], tau, SCALE, None, ALU.mult).then_inc(taus_done, 1)
            dve.wait_ge(taus_done, 1)
            for b in range(BATCH):
                ins = nc.vector.tensor_scalar(bqs[:, b], bq, taus[:, b:b + 1], None, ALU.mult)
            ins.then_inc(bqs_done, 1)
            dve.wait_ge(delta_in, 16)
            nc.vector.tensor_scalar(delta[96:98], delta[96:98], SCALE, None, ALU.mult).then_inc(delta_scaled, 1)
            dve.wait_ge(delta_scaled, 1)
            nc.vector.tensor_copy(delta_hi[96:98].bitcast(f32r), delta[96:98]).then_inc(delta_split, 1)
            dve.wait_ge(delta_split, 1)
            nc.vector.scalar_tensor_tensor(out=delta_rows[96:98], in0=delta_hi[96:98], scalar=low_row[96:98, 0:1],
                                           in1=delta[96:98], op0=ALU.mult, op1=ALU.add).then_inc(delta_split, 1)
            for l in range(LAYERS):
                for item in BETWEEN if l else BEFORE_0:
                    stage(*item)
                for b in range(BATCH):
                    r = BATCH * l + b
                    for step in range(HEADS):
                        if b + 1 < BATCH:
                            front(r + 1, step)
                        inverts, norm, out_step = finish_steps(r)
                        if step in inverts and b:
                            invert(r - 1, inverts.index(step))
                        if step == norm and b:
                            normalise(r - 1)
                        if step == out_step and b:
                            residual(r - 1)
                        for name, rb in routing(r, step):
                            route(name, rb)
                        for item in norm_after_next(r, step):
                            stage(*item)
                        for item in BESIDE.get((r, step), []):
                            stage(*item)
                    if r == 1:
                        ffn_weights()
            for quarter in range(4):
                invert(ROUNDS - 1, quarter)
            normalise(ROUNDS - 1)
            for name, b in LATE:
                if name == "output":
                    residual(BATCH + b)
                else:
                    route(name, b)
            block_table()
            take_up(0, 0)
            moe_blocks(0, first=True)
            moe_blocks(1)
            with dve.Fori(2, TURNS - 1) as turn:
                moe_blocks(turn)
            e = moe_blocks(TURNS - 1, last=True)
            for u in (UNROLL - 2, UNROLL - 1):
                finish(BLOCKS - UNROLL + u, u, e[u], TURNS - 1)
            for b in range(BATCH):
                dve.wait_ge(yt_in[b], 16)
                y = yt[:, b].rearrange("p (t k d) -> p t k d", t=TILES, k=TOPK)
                nc.vector.tensor_tensor(x[:, b], x[:, b], y[:, :, 0], ALU.add).then_inc(first_added, 1)
                dve.wait_ge(first_added, b + 1)
                nc.vector.tensor_tensor(x[:, b], x[:, b], y[:, :, 1], ALU.add).then_inc(x_final, 1)

        @block.tensor
        def _(pe):
            def transposes(src, *u):
                for t in range(TILES):
                    ins = nc.tensor.transpose(bank(*u)[:, 128 * t:128 * t + 128], src[:, t], ident[:])
                fills(ins, *u)

            def front(r, step):
                for what, *which in front_at(r, step):
                    front_part(r, what, *which)

            def front_part(r, what, *which):
                s, l, b = r % 2, r // BATCH, r % BATCH
                if what == "q":
                    c, = which
                    if c == 0:
                        wait_drained(pe, "tr", r)
                    wait_bank(pe, "q", r, c)
                    fills(nc.tensor.matmul(bank("q", r, c), wq[:, l, c], xt[:, s], start=True, stop=True), "q", r, c)
                elif what == "a":
                    c, t = which
                    if t == 0:
                        wait_drained(pe, "q", r, c)
                    if t == 0 and c == 0:
                        pe.wait_ge(ks_even, r + 1)
                        pe.wait_ge(ks_odd, r + 1)
                    if t == 0 and c == 0 and r == 0:
                        pe.wait_ge(sel_in, 16)
                        pe.wait_ge(delta_rep, 16 * BATCH)
                        pe.wait_ge(ones_set, 7)
                    wait_bank(pe, "a", r, c, t)
                    fills(nc.tensor.matmul(bank("a", r, c, t)[:, 0:PER_GROUP * CTX],
                                           qs[0:98, s, c, 128 * t:128 * t + 128],
                                           ks[0:98, b, c].rearrange("p j k -> p (j k)"),
                                           start=True, stop=True), "a", r, c, t)
                else:
                    wait_drained(pe, "a", r, GROUPS - 1, TILES - 1)
                    wait_bank(pe, "mt", r)
                    transposes(maxima[:, s], "mt", r)

            def scores(r, step):
                s, l, b, g = r % 2, r // BATCH, r % BATCH, HEADS * r + step
                j, c = step // GROUPS, step % GROUPS
                if step == 0:
                    wait_drained(pe, "mt", r)
                if step == 1:
                    pe.wait_ge(max_rep, 16 * (r + 1))
                if g >= 2:
                    pe.wait_ge(exp_done, g - 1)
                nc.tensor.matmul(sc[0:CTX, g % 2], ks[0:STACK, b, c, j], qs[0:STACK, s, c],
                                 start=True, stop=True).then_inc(scores_ready, 1)

            def values(r, j, which):
                l, b, g = r // BATCH, r % BATCH, HEADS * r + GROUPS * j
                if which == "num":
                    if j == 0 and r:
                        pe.wait_ge(num_copied, r)
                    pe.wait_ge(exp_done, g + GROUPS)
                elif j == 0 and r:
                    pe.wait_ge(den_copied, r)
                for c in range(GROUPS):
                    out = num_den[32 * c:32 * c + 32, 0 if which == "num" else 1]
                    w = vm[:, b, PER_GROUP * c + j] if which == "num" else ones_v[:, j]
                    ins = nc.tensor.matmul(out, w, probs[:, (g + c) % PROB_SLOTS], start=(j == 0),
                                           stop=(j == PER_GROUP - 1), tile_position=(0, 32 * c))
                if which == "den":
                    ins.then_inc(den_ready, 1)
                elif j == PER_GROUP - 1:
                    ins.then_inc(num_ready, 1)

            def values_at(r, step):
                for which, lag in (("num", NUM_STEP), ("den", DEN_STEP)):
                    if (step - lag) % GROUPS == 0:
                        j = (step - lag) // GROUPS
                        if j >= 0:
                            values(r, j, which)
                        elif r % BATCH:
                            values(r - 1, PER_GROUP + j, which)

            def output(r):
                pe.wait_ge(ot_done, r + 1)
                wait_bank(pe, "o", r)
                for t in range(TILES):
                    ins = nc.tensor.matmul(bank("o", r)[:, 128 * t:128 * t + 128], ot[:, 128 * t:128 * t + 128],
                                           wo[:, r // BATCH], start=True, stop=True)
                fills(ins, "o", r)

            def route(stage, b):
                if stage == "transpose":
                    pe.wait_ge(xm_done, b + 1)
                    wait_bank(pe, "rt", b)
                    transposes(xm[:, b % 2, :, 0:DIM], "rt", b)
                elif stage == "logits":
                    if b == 0:
                        pe.wait_ge(moe_in, 16 * MOE_DMAS)
                    wait_drained(pe, "rt", b)
                    wait_bank(pe, "rl", b)
                    for t in range(TILES):
                        ins = nc.tensor.matmul(bank("rl", b)[:, EXPERTS * t:EXPERTS * t + EXPERTS],
                                               xtm[:, 128 * t:128 * t + 128], gate[:], start=True, stop=True)
                    fills(ins, "rl", b)
                elif stage == "count":
                    pe.wait_ge(selected, b + 1)
                    wait_bank(pe, "rc", b)
                    either = chosen[:, b % 2, TOPK].rearrange("p t e -> p (t e)")
                    nc.tensor.matmul(bank("rc", b)[:, 0:TILES * EXPERTS], before[:], either, start=True, stop=True)
                    fills(nc.tensor.matmul(bank("rc", b)[:, TILES * EXPERTS:2 * TILES * EXPERTS], all_ones[:], either,
                                           start=True, stop=True), "rc", b)

            def turn_rows(n, u, turn):
                pe.wait_ge(rows_in[u], 16 * (turn + 1))
                wait(pe, xs_done, n - 1)
                nc.tensor.transpose(ring[:, u % 2, 0:128], rows[:, u, 0:DIM], ident[:]).then_inc(x_ready, 1)

            def first_product(n, u, e):
                pe.wait_ge(xs_done, n + 1)
                wait(pe, zs_done, n - 1)
                nc.tensor.matmul(ring[:, 2 + u % 2], xs[:, u % 2], w1[:, bass.ds(e * FF, FF)], start=True,
                                 stop=True).then_inc(z_ready, 1)

            def turn_hidden(n, u):
                pe.wait_ge(zs_done, n + 1)
                wait(pe, ht_done, n - 1)
                for i in range(FF_BLOCKS):
                    ins = nc.tensor.transpose(num_den[:, u % 2, 128 * i:128 * i + 128], zs[:, u % 2, 128 * i:128 * i + 128],
                                              ident[:])
                ins.then_inc(zt_ready, 1)

            def second_product(n, u, e):
                pe.wait_ge(ht_done, n + 1)
                wait(pe, ys_done, n - 1)
                for i in range(FF_BLOCKS):
                    ins = nc.tensor.matmul(sc[:, u % 2, 0:DIM], ht[:, u % 2, i], w2[:, bass.ds(e * FF + i * DIM, DIM)],
                                           start=(i == 0), stop=(i == FF_BLOCKS - 1))
                ins.then_inc(y_ready, 1)

            def moe_blocks(turn, first=False, last=False):
                n0 = turn * UNROLL
                e = experts_of(pe, turn)
                for u in range(UNROLL):
                    first_product(n0 + u, u, e[u])
                    if not (last and u == UNROLL - 1):
                        turn_rows(n0 + u + 1, (u + 1) % UNROLL, turn + (u + 1) // UNROLL)
                    if not (first and u == 0):
                        turn_hidden(n0 + u - 1, (u - 1) % UNROLL)
                    if not (first and u < 2):
                        second_product(n0 + u - 2, (u - 2) % UNROLL, e[u - 2])
                return e

            def keep_warm(products):
                for _ in range(products):
                    nc.tensor.matmul(sc[:, 0], zeros[:, 0:128], zeros[:], start=True, stop=True)

            def stage(kind, *which):
                if kind == "front":
                    for step in which[1]:
                        front(which[0], step)
                elif kind == "maxima":
                    for step in which[1]:
                        for w in front_at(which[0], step):
                            if w[0] == "a":
                                front_part(which[0], *w)
                elif kind == "q":
                    front_part(which[0], "q", which[1])
                elif kind == "warm":
                    keep_warm(*which)
                elif kind == "tr":
                    r, = which
                    wait_xn(pe, ln_of_round(r))
                    wait_bank(pe, "tr", r)
                    transposes(xn[:, r % 2], "tr", r)
                elif kind == "k":
                    l, c = which
                    if c == 0:
                        pe.wait_ge(key_in, 16 * KEY_DMAS) if l == 0 else pe.wait_ge(ffn_in, 16 * FFN_DMAS)
                    wait_bank(pe, "k", l, c)
                    fills(nc.tensor.matmul(bank("k", l, c)[:, 0:CTX_ALL], wk[:, l, c], ctx_t[:],
                                           start=True, stop=True), "k", l, c)
                elif kind == "v":
                    l, b = which
                    if l == 0 and b == 0:
                        pe.wait_ge(value_in, 16 * VALUE_DMAS)
                    wait_bank(pe, "v", l, b)
                    fills(nc.tensor.matmul(bank("v", l, b)[0:CTX, 0:128], ctx_t[:, b * CTX:(b + 1) * CTX], wv[:, l],
                                           start=True, stop=True), "v", l, b)
                elif kind == "ftr":
                    b, = which
                    wait_xn(pe, BATCH + b)
                    wait_bank(pe, "ftr", b)
                    transposes(xn[:, b % 2], "ftr", b)
                elif kind == "fp":
                    b, = which
                    wait_drained(pe, "ftr", b)
                    wait_bank(pe, "fp", b)
                    fills(nc.tensor.matmul(bank("fp", b), u1[:], xt[:, b % 2], start=True, stop=True), "fp", b)
                elif kind == "hidden":
                    b, = which
                    if b == 0:
                        pe.wait_ge(v1_split, 3)
                        pe.wait_ge(exp_done, HEADS * BATCH)
                        pe.wait_ge(num_copied, BATCH)
                        pe.wait_ge(den_copied, BATCH)
                    wait_drained(pe, "fp", b)
                    for i in range(FF_BLOCKS):
                        if b:
                            pe.wait_ge(h_done, FF_BLOCKS * (b - 1) + i + 1)
                        nc.tensor.matmul(hbank(i), v1s[0:96, 128 * i:128 * i + 128], pstack[0:96, b % 3],
                                         start=True, stop=True).then_inc(h_ready, 1)
                elif kind == "o":
                    output(BATCH - 1)
                elif kind == "fq":
                    b, = which
                    wait_bank(pe, "fq", b)
                    pe.wait_ge(h_done, FF_BLOCKS * (b + 1))
                    for i in range(FF_BLOCKS):
                        ins = nc.tensor.matmul(bank("fq", b)[32 * i:32 * i + 32], u2[:, i], hid[:, b % 2, i],
                                               start=True, stop=True, tile_position=(0, 32 * i))
                    fills(ins, "fq", b)
                elif kind == "fo":
                    b, = which
                    wait_drained(pe, "fq", b)
                    wait_bank(pe, "fo", b)
                    for t in range(TILES):
                        ins = nc.tensor.matmul(bank("fo", b)[:, 128 * t:128 * t + 128], q4[:, 128 * t:128 * t + 128],
                                               v2[:], start=True, stop=True)
                    fills(ins, "fo", b)

            pe.wait_ge(zeros_set, 1)
            keep_warm(WARM_BEFORE)
            pe.wait_ge(query_in, 16 * QUERY_DMAS)
            for l in range(LAYERS):
                for item in BETWEEN if l else BEFORE_0:
                    stage(*item)
                if l:
                    pe.wait_ge(h_done, FF_BLOCKS * BATCH)
                for b in range(BATCH):
                    r = BATCH * l + b
                    for step in range(HEADS):
                        scores(r, step)
                        if b + 1 < BATCH:
                            front(r + 1, step)
                        values_at(r, step)
                        if step == finish_steps(r)[2] and b:
                            output(r - 1)
                        for name, rb in routing(r, step):
                            route(name, rb)
                        for item in BESIDE.get((r, step), []):
                            stage(*item)
                r = BATCH * l + BATCH - 1
                values(r, PER_GROUP - 1, "num")
                values(r, PER_GROUP - 1, "den")
            for name, b in LATE:
                if name == "output":
                    output(BATCH + b)
                elif name == "warm":
                    keep_warm(b)
                else:
                    route(name, b)
            keep_warm(WARM_MOE)
            pe.wait_ge(table_done, 1)
            turn_rows(0, 0, 0)
            moe_blocks(0, first=True)
            with pe.Fori(1, TURNS - 1) as turn:
                moe_blocks(turn)
            e = moe_blocks(TURNS - 1, last=True)
            turn_hidden(BLOCKS - 1, UNROLL - 1)
            for u in (UNROLL - 2, UNROLL - 1):
                second_product(BLOCKS - UNROLL + u, u, e[u])


def arrays_for(inputs):
    a = {k: np.asarray(v) for k, v in inputs.items()}
    rep = {}
    cols = np.array([[8 * (PER_GROUP * c) + i % 32 for i in range(128)] for c in range(GROUPS)])
    def stacked(l, name):
        w = a[f"L{l}_xcond_W{name}"]
        return w[cols].transpose(2, 0, 1)
    def stacked_bias(l, name):
        return a[f"L{l}_xcond_b{name}"][cols].T
    rows = lambda v: np.broadcast_to(v, (128, v.shape[-1]))
    layers = range(LAYERS)
    rep["ident"] = np.eye(128, dtype=np.float32)
    rep["x"] = a["x"].reshape(BATCH, 128, TILES, DIM)
    rep["ctx_t"] = a["ctx_1024"].reshape(CTX_ALL, DIM).T
    rep["delta"] = a["fside_BxS2_0"].reshape(1, CTX_ALL)
    j = (np.arange(128) % 32) // 8
    member = (j[:, None] == np.arange(PER_GROUP)[None]).astype(np.float32)
    low_row = -(np.arange(128) == 97).astype(np.float32)[:, None]
    own_columns = np.arange(32)[None] // HEAD_DIM == np.arange(PER_GROUP)[:, None]
    rep["ones_v"] = ((np.arange(128) < CTX)[:, None, None] & own_columns[None]).astype(np.float32)
    sel = -(np.arange(HEADS)[:, None] == np.arange(HEADS)[None]).astype(np.float32)
    rep["minus_sel"] = np.broadcast_to(sel.reshape(HEADS, 1, GROUPS, PER_GROUP, 1), (HEADS, BATCH, GROUPS, PER_GROUP, CTX))
    rep["wq"] = np.stack([stacked(l, "q") for l in layers], 1)
    rep["wk"] = np.stack([stacked(l, "k") for l in layers], 1)
    rep["wv"] = np.stack([a[f"L{l}_xcond_Wv"].T for l in layers], 1)
    rep["wo"] = np.stack([a[f"L{l}_xcond_Wo"].T for l in layers], 1)
    rep["small"] = np.concatenate([stacked_bias(l, "q") for l in layers] + [stacked_bias(l, "k") for l in layers] +
                                  [member, rows(a["condB_tau"].reshape(1, BATCH)), a["L0_ffn_b1"].reshape(FF_BLOCKS, 128).T,
                                   low_row], 1)
    rep["wide"] = np.stack([rows(a[f"L{l}_xcond_b{name}"]) for name in "vo" for l in layers] + [rows(a["L0_ffn_b2"])], 1)
    rep["u1"] = np.tile(a["L0_ffn_U1"], (1, 4))
    rep["v1"] = np.tile(a["L0_ffn_V1"], (3, 1))
    rep["u2"] = a["L0_ffn_U2"].reshape(FF_BLOCKS, 128, RANK).transpose(1, 0, 2)
    rep["v2"] = np.tile(a["L0_ffn_V2"], (4, 1))
    rep["gate"] = a["L1_ffn_gate_w"].T
    rep["w1"] = a["L1_ffn_w1"].transpose(1, 0, 2).reshape(128, EXPERTS * FF)
    rep["w2"] = a["L1_ffn_w2"].reshape(EXPERTS * FF_BLOCKS, 128, DIM).transpose(1, 0, 2).reshape(128, -1)
    rep["e_b1"] = a["L1_ffn_b1"].reshape(EXPERTS * FF_BLOCKS, 128).T
    rep["e_b2"] = rows(a["L1_ffn_b2"].reshape(1, -1))
    rep["before"] = np.triu(np.ones((128, 128), np.float32), 1)
    rep["tie"] = rows(np.tril(np.ones((EXPERTS, EXPERTS), np.float32), -1).reshape(1, -1))
    blocks = np.arange(BLOCKS)
    rep["iota"] = np.concatenate([blocks, 128 * blocks, 8 ** (blocks % UNROLL), 128 * np.arange(16)])[None].astype(np.float32)
    rep["regions"] = rows((REGION * np.arange(EXPERTS))[None].astype(np.float32))
    token = SEQ * np.arange(BATCH)[None, :, None] + TILES * np.arange(128)[:, None, None] + np.arange(TILES)
    rep["second_at"] = (TOPK * token + 1).astype(np.float32).reshape(128, TOKEN_TILES)
    pad = np.zeros(((EXPERTS + SPARE) * 128, ROW), np.float32)
    pad[:, GOES:GOES + EXPERTS] = TOKENS * TOPK + np.arange(len(pad))[:, None]
    rep["pad_rows"] = pad
    return {k: np.ascontiguousarray(v) for k, v in rep.items()}


def kernel(**inputs):
    import concourse.bacc as bacc
    from concourse.bass_utils import run_bass_kernel_spmd

    nc = bacc.Bacc("TRN2", target_bir_lowering=False, num_devices=1)
    arrays = {f"in_{k}": v for k, v in arrays_for(inputs).items()}
    io = {k[3:]: nc.dram_tensor(k, v.shape, mybir.dt.from_np(v.dtype), kind="ExternalInput").ap() for k, v in arrays.items()}
    out = nc.dram_tensor("out", (BATCH, 128, TILES, DIM), mybir.dt.float32, kind="ExternalOutput").ap()
    pixart_blocks(nc, io, out)
    r = run_bass_kernel_spmd(nc, [arrays], core_ids=[0])
    return r.results[0]["out"].reshape(BATCH, SEQ, DIM)
```
